# Optimizing a Trainium2 kernel written in Bass

```python
import numpy as np
import jax
import jax.numpy as jnp

def _softmax(x, axis=-1):
    return jax.nn.softmax(x, axis=axis)

def _gelu(x):
    return jax.nn.gelu(x, approximate=True)

def _silu(x):
    return jax.nn.silu(x)

def _sigmoid(x):
    return jax.nn.sigmoid(x)

def _layernorm(x, axis=-1, eps=1e-05):
    m = jnp.mean(x, axis=axis, keepdims=True)
    v = jnp.var(x, axis=axis, keepdims=True)
    return (x - m) / jnp.sqrt(v + eps)

def _scatter_add(tgt, idx, src, axis=0):
    return tgt.at[idx].add(src)

def _segment_sum(src, seg, n):
    return jax.ops.segment_sum(src, seg, n)
kernel_name = 'mk_vit_tower_d1_tok_img768_r4_d4f4e7'

def setup_inputs(seed: int=0):
    np.random.seed(seed)
    _w = jnp.asarray

    def _rec_inputs():
        import jax
        import jax.numpy as jnp
        _rk = jax.random.key(seed)
        x = -0.000356955 + 1 * jax.random.normal(jax.random.fold_in(_rk, 1), (128, 3, 224, 224), jnp.float32)
        return x
    x = _rec_inputs()

    def _L0_tok_setup():
        import jax, jax.numpy as jnp
        import numpy as np
        N_PATCHES = 14
        HIDDEN_D = 192
        N_HEADS = 12
        D_HEAD = HIDDEN_D // N_HEADS
        SEQ = N_PATCHES ** 2 + 1
        INPUT_D = 3 * 16 * 16
        LN_EPS = 1e-05

        def positional_embeddings(seq_len, d):
            i = jnp.arange(seq_len, dtype=jnp.float32)[:, None]
            j = jnp.arange(d, dtype=jnp.float32)[None, :]
            even = (jnp.arange(d) % 2 == 0)[None, :]
            denom_even = jnp.power(10000.0, j / d)
            denom_odd = jnp.power(10000.0, (j - 1.0) / d)
            return jnp.where(even, jnp.sin(i / denom_even), jnp.cos(i / denom_odd))

        def _forward(images, W_map, b_map, class_token, ln_w, ln_b, Wq, bq, Wk, bk, Wv, bv):
            n = images.shape[0]
            patches = images.reshape(n, N_PATCHES ** 2, INPUT_D)
            tokens = jnp.einsum('npi,di->npd', patches, W_map) + b_map
            cls = jnp.broadcast_to(class_token[None], (n, 1, HIDDEN_D))
            tokens = jnp.concatenate([cls, tokens], axis=1)
            tokens = tokens + positional_embeddings(SEQ, HIDDEN_D)[None]
            mean = jnp.mean(tokens, axis=(-2, -1), keepdims=True)
            var = jnp.var(tokens, axis=(-2, -1), keepdims=True)
            x = (tokens - mean) / jnp.sqrt(var + LN_EPS) * ln_w + ln_b
            xh = x.reshape(n, SEQ, N_HEADS, D_HEAD)
            q = jnp.einsum('bshd,hed->bshe', xh, Wq) + bq[None, None]
            k = jnp.einsum('bshd,hed->bshe', xh, Wk) + bk[None, None]
            v = jnp.einsum('bshd,hed->bshe', xh, Wv) + bv[None, None]
            att = jax.nn.softmax(jnp.einsum('bshd,bthd->bhst', q, k) / jnp.sqrt(jnp.float32(D_HEAD)), axis=-1)
            msa = jnp.einsum('bhst,bthd->bshd', att, v).reshape(n, SEQ, HIDDEN_D)
            return tokens + msa
        key = jax.random.key(seed)
        ks = jax.random.split(key, 12)
        s = 0.02
        return {'images': jax.random.normal(ks[0], (128, 3, 224, 224), dtype=jnp.float32), 'W_map': jax.random.normal(ks[1], (HIDDEN_D, INPUT_D), dtype=jnp.float32) * s, 'b_map': jax.random.normal(ks[2], (HIDDEN_D,), dtype=jnp.float32) * s, 'class_token': jax.random.uniform(ks[3], (1, HIDDEN_D), dtype=jnp.float32), 'ln_w': jnp.ones((SEQ, HIDDEN_D), dtype=jnp.float32), 'ln_b': jnp.zeros((SEQ, HIDDEN_D), dtype=jnp.float32), 'Wq': jax.random.normal(ks[4], (N_HEADS, D_HEAD, D_HEAD), dtype=jnp.float32) * s, 'bq': jax.random.normal(ks[5], (N_HEADS, D_HEAD), dtype=jnp.float32) * s, 'Wk': jax.random.normal(ks[6], (N_HEADS, D_HEAD, D_HEAD), dtype=jnp.float32) * s, 'bk': jax.random.normal(ks[7], (N_HEADS, D_HEAD), dtype=jnp.float32) * s, 'Wv': jax.random.normal(ks[8], (N_HEADS, D_HEAD, D_HEAD), dtype=jnp.float32) * s, 'bv': jax.random.normal(ks[9], (N_HEADS, D_HEAD), dtype=jnp.float32) * s}
    _L0_tok_all = _L0_tok_setup()
    _L0_tok_in = {k: v for k, v in _L0_tok_all.items() if k in ('W_map', 'b_map', 'class_token', 'ln_w', 'ln_b', 'Wq', 'bq', 'Wk', 'bk', 'Wv', 'bv')}
    del _L0_tok_all

    def _L0_attn_setup():
        import jax, jax.numpy as jnp
        import numpy as np
        N_HEAD = 12
        key = jax.random.key(seed)
        k1, k2, k3 = jax.random.split(key, 3)
        nx = 192
        B, S = (2, 512)
        return {'hidden_states': jax.random.normal(k1, (B, S, nx), dtype=jnp.float32), 'w_attn': jax.random.normal(k2, (nx, 3 * nx), dtype=jnp.float32) * 0.02, 'b_attn': jnp.zeros((3 * nx,), dtype=jnp.float32), 'w_proj': jax.random.normal(k3, (nx, nx), dtype=jnp.float32) * 0.02, 'b_proj': jnp.zeros((nx,), dtype=jnp.float32)}
    _L0_attn_all = _L0_attn_setup()
    _L0_attn_in = {k: v for k, v in _L0_attn_all.items() if k in ('w_attn', 'b_attn', 'w_proj', 'b_proj')}
    del _L0_attn_all

    def _L0_ffn_setup():
        import jax, jax.numpy as jnp
        import numpy as np
        HIDDEN = 192
        INNER = 128
        EPS = 1e-05
        key = jax.random.key(seed)
        ks = jax.random.split(key, 6)
        B, S = (8, 1024)
        x = jax.random.normal(ks[0], (B, S, HIDDEN), dtype=jnp.float32)
        W1 = jax.random.normal(ks[1], (INNER, HIDDEN), dtype=jnp.float32) * 0.02
        b1 = jnp.zeros((INNER,), dtype=jnp.float32)
        W2 = jax.random.normal(ks[2], (HIDDEN, INNER), dtype=jnp.float32) * 0.02
        b2 = jnp.zeros((HIDDEN,), dtype=jnp.float32)
        bound = 1.0 / np.sqrt(HIDDEN)
        Wo = jax.random.uniform(ks[3], (HIDDEN, HIDDEN), minval=-bound, maxval=bound, dtype=jnp.float32)
        bo = jax.random.uniform(ks[4], (HIDDEN,), minval=-bound, maxval=bound, dtype=jnp.float32)
        gamma = jnp.ones((HIDDEN,), dtype=jnp.float32)
        beta = jnp.zeros((HIDDEN,), dtype=jnp.float32)
        return {'x': x, 'W1': W1, 'b1': b1, 'W2': W2, 'b2': b2, 'Wo': Wo, 'bo': bo, 'gamma': gamma, 'beta': beta}
    _L0_ffn_all = _L0_ffn_setup()
    _L0_ffn_in = {k: v for k, v in _L0_ffn_all.items() if k in ('W1', 'b1', 'W2', 'b2', 'Wo', 'bo', 'gamma', 'beta')}
    del _L0_ffn_all
    return {'x': x, 'L0_tok_W_map': _L0_tok_in['W_map'], 'L0_tok_b_map': _L0_tok_in['b_map'], 'L0_tok_class_token': _L0_tok_in['class_token'], 'L0_tok_ln_w': _L0_tok_in['ln_w'], 'L0_tok_ln_b': _L0_tok_in['ln_b'], 'L0_tok_Wq': _L0_tok_in['Wq'], 'L0_tok_bq': _L0_tok_in['bq'], 'L0_tok_Wk': _L0_tok_in['Wk'], 'L0_tok_bk': _L0_tok_in['bk'], 'L0_tok_Wv': _L0_tok_in['Wv'], 'L0_tok_bv': _L0_tok_in['bv'], 'L0_attn_w_attn': _L0_attn_in['w_attn'], 'L0_attn_b_attn': _L0_attn_in['b_attn'], 'L0_attn_w_proj': _L0_attn_in['w_proj'], 'L0_attn_b_proj': _L0_attn_in['b_proj'], 'L0_ffn_W1': _L0_ffn_in['W1'], 'L0_ffn_b1': _L0_ffn_in['b1'], 'L0_ffn_W2': _L0_ffn_in['W2'], 'L0_ffn_b2': _L0_ffn_in['b2'], 'L0_ffn_Wo': _L0_ffn_in['Wo'], 'L0_ffn_bo': _L0_ffn_in['bo'], 'L0_ffn_gamma': _L0_ffn_in['gamma'], 'L0_ffn_beta': _L0_ffn_in['beta']}

def reference(x, L0_tok_W_map, L0_tok_b_map, L0_tok_class_token, L0_tok_ln_w, L0_tok_ln_b, L0_tok_Wq, L0_tok_bq, L0_tok_Wk, L0_tok_bk, L0_tok_Wv, L0_tok_bv, L0_attn_w_attn, L0_attn_b_attn, L0_attn_w_proj, L0_attn_b_proj, L0_ffn_W1, L0_ffn_b1, L0_ffn_W2, L0_ffn_b2, L0_ffn_Wo, L0_ffn_bo, L0_ffn_gamma, L0_ffn_beta):
    import jax
    import jax.numpy as jnp

    def _L0_tok_ref(images, W_map, b_map, class_token, ln_w, ln_b, Wq, bq, Wk, bk, Wv, bv):
        import jax, jax.numpy as jnp
        import numpy as np
        N_PATCHES = 14
        HIDDEN_D = 192
        N_HEADS = 12
        D_HEAD = HIDDEN_D // N_HEADS
        SEQ = N_PATCHES ** 2 + 1
        INPUT_D = 3 * 16 * 16
        LN_EPS = 1e-05

        def positional_embeddings(seq_len, d):
            i = jnp.arange(seq_len, dtype=jnp.float32)[:, None]
            j = jnp.arange(d, dtype=jnp.float32)[None, :]
            even = (jnp.arange(d) % 2 == 0)[None, :]
            denom_even = jnp.power(10000.0, j / d)
            denom_odd = jnp.power(10000.0, (j - 1.0) / d)
            return jnp.where(even, jnp.sin(i / denom_even), jnp.cos(i / denom_odd))

        def _forward(images, W_map, b_map, class_token, ln_w, ln_b, Wq, bq, Wk, bk, Wv, bv):
            n = images.shape[0]
            patches = images.reshape(n, N_PATCHES ** 2, INPUT_D)
            tokens = jnp.einsum('npi,di->npd', patches, W_map) + b_map
            cls = jnp.broadcast_to(class_token[None], (n, 1, HIDDEN_D))
            tokens = jnp.concatenate([cls, tokens], axis=1)
            tokens = tokens + positional_embeddings(SEQ, HIDDEN_D)[None]
            mean = jnp.mean(tokens, axis=(-2, -1), keepdims=True)
            var = jnp.var(tokens, axis=(-2, -1), keepdims=True)
            x = (tokens - mean) / jnp.sqrt(var + LN_EPS) * ln_w + ln_b
            xh = x.reshape(n, SEQ, N_HEADS, D_HEAD)
            q = jnp.einsum('bshd,hed->bshe', xh, Wq) + bq[None, None]
            k = jnp.einsum('bshd,hed->bshe', xh, Wk) + bk[None, None]
            v = jnp.einsum('bshd,hed->bshe', xh, Wv) + bv[None, None]
            att = jax.nn.softmax(jnp.einsum('bshd,bthd->bhst', q, k) / jnp.sqrt(jnp.float32(D_HEAD)), axis=-1)
            msa = jnp.einsum('bhst,bthd->bshd', att, v).reshape(n, SEQ, HIDDEN_D)
            return tokens + msa
        return _forward(images, W_map, b_map, class_token, ln_w, ln_b, Wq, bq, Wk, bk, Wv, bv)

    def _L0_attn_ref(hidden_states, w_attn, b_attn, w_proj, b_proj):
        import jax, jax.numpy as jnp
        import numpy as np
        N_HEAD = 12
        B, S, nx = hidden_states.shape
        d_head = nx // N_HEAD
        qkv = hidden_states @ w_attn + b_attn
        q, k, v = jnp.split(qkv, 3, axis=-1)

        def split(x):
            return x.reshape(B, S, N_HEAD, d_head).transpose(0, 2, 1, 3)
        q, k, v = (split(q), split(k), split(v))
        w = jnp.einsum('bhsd,bhtd->bhst', q, k) / jnp.sqrt(jnp.float32(d_head))
        w = jax.nn.softmax(w, axis=-1)
        a = jnp.einsum('bhst,bhtd->bhsd', w, v)
        a = a.transpose(0, 2, 1, 3).reshape(B, S, nx)
        return a @ w_proj + b_proj

    def _L0_ffn_ref(x, W1, b1, W2, b2, Wo, bo, gamma, beta):
        import jax, jax.numpy as jnp
        import numpy as np
        HIDDEN = 192
        INNER = 128
        EPS = 1e-05
        h = jax.nn.relu(jnp.einsum('bsd,id->bsi', x, W1) + b1)
        pred = jnp.einsum('bsi,di->bsd', h, W2) + b2
        out = jnp.einsum('bsd,ed->bse', pred, Wo) + bo
        mu = jnp.mean(out, axis=-1, keepdims=True)
        var = jnp.mean(jnp.square(out - mu), axis=-1, keepdims=True)
        out = (out - mu) * jax.lax.rsqrt(var + EPS) * gamma + beta
        return out
    h = _L0_tok_ref(x, L0_tok_W_map, L0_tok_b_map, L0_tok_class_token, L0_tok_ln_w, L0_tok_ln_b, L0_tok_Wq, L0_tok_bq, L0_tok_Wk, L0_tok_bk, L0_tok_Wv, L0_tok_bv)
    h = h + _L0_attn_ref(_layernorm(h, axis=-1), L0_attn_w_attn, L0_attn_b_attn, L0_attn_w_proj, L0_attn_b_proj)
    h = h + _L0_ffn_ref(_layernorm(h, axis=-1), L0_ffn_W1, L0_ffn_b1, L0_ffn_W2, L0_ffn_b2, L0_ffn_Wo, L0_ffn_bo, L0_ffn_gamma, L0_ffn_beta)
    return h

_drawn_inputs = setup_inputs


def setup_inputs(seed=0):
    import zlib

    import numpy as np

    out = dict(_drawn_inputs(seed))
    spreads = {'L0_tok_ln_w': (1.0, 0.6),
     'L0_tok_ln_b': (0.0, 2.0),
     'L0_attn_b_attn': (0.0, 0.35),
     'L0_attn_b_proj': (0.0, 0.1),
     'L0_ffn_b1': (0.0, 0.1),
     'L0_ffn_b2': (0.0, 0.1),
     'L0_ffn_gamma': (1.0, 0.2),
     'L0_ffn_beta': (0.0, 0.1)}
    factors = {'L0_tok_b_map': 3.402,
     'L0_tok_class_token': 3.251,
     'L0_tok_Wq': 8.0,
     'L0_tok_bq': 43.841,
     'L0_tok_Wk': 8.0,
     'L0_tok_bk': 64.0,
     'L0_tok_bv': 3.537}
    for name, (base, spread) in spreads.items():
        noise = np.random.default_rng([zlib.crc32(name.encode()), seed]).standard_normal(out[name].shape)
        drawn = base * np.exp(spread * noise) if base else spread * noise
        out[name] = jnp.asarray(drawn.astype(out[name].dtype))
    for name, factor in factors.items():
        out[name] = (out[name] * factor).astype(out[name].dtype)
    return out
```

```python
from contextlib import ExitStack

import concourse.bass as bass
from concourse import mybir

F32 = mybir.dt.float32
BF16 = mybir.dt.bfloat16
ALU = mybir.AluOpType
ACT = mybir.ActivationFunctionType
AX = mybir.AxisListType

P = 128
IMGS = 2
S = 197
D = 192
HEADS = 12
DH = D // HEADS
DB = D - P
PIX = 768
CH = PIX // P
INNER = 128
LN_EPS = 1e-5
ROWS = [P, S - P]
COLS = [slice(0, P), slice(P, S)]
NT = 2 * IMGS
W = IMGS * S
PARTS = 3
SLOT_Q = [0, 0, 0, 1, 1, 2]
SLOT_K = [0, 1, 2, 0, 1, 0]
KS = len(SLOT_Q) * DH
KM = KS + PARTS
QUADS = IMGS * HEADS // 4
STEPS = 4 * QUADS
HG = 8

_SIZES = [("wm", CH * D), ("pos", 2 * D), ("tokb", 2 * D), ("lnw", 2 * D), ("lnb", 2 * D),
          ("g1", 2 * 3 * P), ("g2", 2 * 3 * P), ("gb1", 3), ("gb2", 3), ("wv1", 2 * D),
          ("wv2", 2 * D), ("wp", 2 * D), ("w1", 2 * INNER), ("w2", 2 * INNER), ("wo", 2 * D),
          ("b2", 2 * P), ("gam", D), ("bet", D), ("ident", P), ("avg", P)]
CONST = {}
_at = 0
for _name, _n in _SIZES:
    CONST[_name] = (_at, _n)
    _at += _n
NCONST = _at

JOBS = ([(f"ot1_{n}", "c1") for n in range(NT)] + [("mt2", "c2")]
        + [(f"emb_{b}", "a") for b in range(IMGS)]
        + [("xt2_0", "c1"), ("xt2_1", "c1"), ("mean", "a")]
        + [("g2_0", "c1"), ("var", "a"), ("g2_1", "c1"), ("g2_2", "c1")] + [("xt1_0", "a"), ("xt1_1", "a")]
        + [(f"g1_{g}", "a") for g in range(3)] + [(f"v1_{b}", "a") for b in range(IMGS)]
        + [(f"ot2_{n}", "c2") for n in range(NT)] + [("mt1", "a")]
        + [(f"v2_{b}", "c1") for b in range(IMGS)]
        + [("at_0", "c2"), ("at_1", "c2")] + [(f"proj_{b}", "c2") for b in range(IMGS)]
        + [("ft_0", "c2"), ("ft_1", "c2"), ("up", "c2")]
        + [(f"down_{b}", "c2") for b in range(IMGS)])
NBANK = 3


class Body:

    def __init__(self, i, c1, c2, a, before, passes, cores):
        self.i, self.c1, self.c2, self.a = i, c1, c2, a
        self.before, self.passes, self.cores = before, passes, cores

    def has(self, unit):
        return {"c1": self.c1, "c2": self.c2, "a": self.a}[unit]

    def jobs_per_bank(self):
        n = [0] * NBANK
        for k, (_, unit) in enumerate(JOBS):
            n[k % NBANK] += self.has(unit)
        return n

    def job(self, name):
        done = list(self.before)
        for k, (other, unit) in enumerate(JOBS):
            done[k % NBANK] = done[k % NBANK] + int(self.has(unit))
            if other == name:
                return k % NBANK, done[k % NBANK]
        raise KeyError(name)


def after(body, times=1):
    return ([x + times * n for x, n in zip(body.before, body.jobs_per_bank())],
            body.passes + times * (body.c2 + body.a), body.cores + times * (body.c1 + body.c2))


def pipeline(eng, units, emit):
    body = Body(-1, False, False, True, [0] * NBANK, 0, 0)
    emit(body)
    body = Body(0, True, False, True, *after(body))
    emit(body)
    body = Body(1, True, True, True, *after(body))
    emit(body)
    start = after(body)
    loops = units - 3
    n = body.jobs_per_bank()
    with eng.Fori(2, 2 + loops) as i:
        emit(Body(i, True, True, True, [x + (i - 2) * m for x, m in zip(start[0], n)],
                  start[1] + (i - 2) * 2, start[2] + (i - 2) * 2))
    body = Body(units - 1, True, True, False, *after(body, 1 + loops))
    emit(body)
    emit(Body(units, False, True, False, *after(body)))


def above(value):
    return not isinstance(value, int) or value > 0


def vit_tower(nc: bass.Bass, x, consts, out):
    units = x.shape[0]
    scratch = [[nc.dram_tensor(f"parts_{o}{s}", (DH * HEADS, PARTS, W), BF16).ap() for o in "qk"]
               for s in (1, 2)]
    scratch_max = [nc.dram_tensor(f"parts_max{s}", (PARTS, HEADS, W), BF16).ap() for s in (1, 2)]

    with ExitStack() as ctx:
        def sb(name, shape, dt=F32):
            return ctx.enter_context(nc.sbuf_tensor(name, shape, dt))

        def bank(name):
            return ctx.enter_context(nc.psum_tensor(name, [P, 512], F32))

        def sem(name):
            return ctx.enter_context(nc.semaphore(name))

        def sem2(name):
            return [sem(f"{name}{s}") for s in (1, 2)]

        const = sb("const", [P, NCONST])

        def c(name, *split):
            at, n = CONST[name]
            v = const[:, at:at + n]
            return v.rearrange("p (a n) -> p a n", a=split[0]) if split else v

        wm, lnw, lnb = c("wm", CH), c("lnw", 2), c("lnb", 2)
        group_w, group_b = [c("g1", 2), c("g2", 2)], [c("gb1"), c("gb2")]
        value_w, proj_w, up_w = [c("wv1", 2), c("wv2", 2)], c("wp", 2), c("w1", 2)
        ident, avg = c("ident"), c("avg")
        pos_bias = sb("pos_bias", [P, 2, D])
        down_w = sb("down_w", [P, D])
        down_b = sb("down_b", [P, D])

        xin = sb("xin", [P, IMGS, CH, S])
        tok = sb("tok", [P, NT, D])
        bst = sb("bst", [P, NT, 6])
        bst1 = sb("bst1", [P, NT, 6])
        mv_img = sb("mv_img", [P, 2, IMGS, 2])
        dev_img = sb("dev_img", [P, 2, IMGS])
        sq_img = sb("sq_img", [P, 2, IMGS])
        e_img = sb("e_img", [P, 2, IMGS])
        mean_img = sb("mean_img", [P, IMGS])
        var_img = sb("var_img", [P, IMGS])
        rstd_img = sb("rstd_img", [P, IMGS])
        xw = sb("xw", [P, NT, D])
        xl = sb("xl", [P, NT, D])
        xT = [[sb(f"xT{s}{k}", [P, IMGS, S]) for k in "AB"] for s in (1, 2)]
        aT = [sb(f"aT{k}", [P, IMGS, S]) for k in "AB"]
        fT = [sb(f"fT{k}", [P, IMGS, S]) for k in "AB"]
        parts = [sb(f"parts{s}", [P, 3, PARTS, W], BF16) for s in (1, 2)]
        rest = [sb(f"rest{s}", [P, 3, W]) for s in (1, 2)]
        stack_q = [sb(f"stack_q{s}", [KM, HEADS, W], BF16) for s in (1, 2)]
        stack_k = [sb(f"stack_k{s}", [KM, HEADS, W], BF16) for s in (1, 2)]
        maxes = sb("maxes", [P, NT, HEADS])
        mparts = [sb(f"mparts{s}", [HEADS, PARTS, W], BF16) for s in (1, 2)]
        mrest = [sb(f"mrest{s}", [HEADS, W]) for s in (1, 2)]
        val = [sb(f"val{s}", [P, NT, HEADS, 2 * DH]) for s in (1, 2)]
        probs = sb("probs", [P, 2, 2, 4, S])
        attT = sb("attT", [P, QUADS, S])
        rden = sb("rden", [P, NT, HEADS])
        att = sb("att", [P, NT, D])
        h1_next = sb("h1_next", [P, NT, D])
        h1 = sb("h1", [P, NT, D])
        mv = sb("mv", [P, NT, 2])
        rstd = sb("rstd", [P, NT])
        var_eps = sb("var_eps", [P, NT])
        spare = sb("spare", [P, 1])
        eps = sb("eps", [P, NT])
        ones = sb("ones", [P, 1])
        minus_half = sb("minus_half", [P, NT])
        xn = sb("xn", [P, NT, D])
        h2 = sb("h2", [P, NT, D])
        h2b = sb("h2b", [P, NT, D])
        hid = sb("hid", [P, IMGS, S])
        y = sb("y", [P, NT, D])
        yn = sb("yn", [P, NT, D])
        yg = sb("yg", [P, NT, D])
        res = sb("res", [P, NT, D])

        mx_bank = [bank("mx_bank0"), bank("mx_bank1")]
        sc_bank = [bank("sc_bank0"), bank("sc_bank1")]
        av_bank = bank("av_bank")
        work = [bank(f"work{k}") for k in range(NBANK)]

        const_in = sem("const_in")
        x_in = sem("x_in")
        parts_out = sem2("parts_out")
        stack_in = sem2("stack_in")
        mparts_out = sem2("mparts_out")
        mrows_in = sem2("mrows_in")
        stored = sem("stored")
        zeroed = sem("zeroed")
        set_up = sem("set_up")
        fold_full = sem("fold_full")
        fold_read = sem("fold_read")
        full = [sem(f"work_full{k}") for k in range(NBANK)]
        read = [sem(f"work_read{k}") for k in range(NBANK)]
        mx_full, mx_read = sem("mx_full"), sem("mx_read")
        sc_full, exp_done = sem("sc_full"), sem("exp_done")
        av_full, av_read = sem("av_full"), sem("av_read")
        high_done = sem2("high_done")
        mid_done = sem2("mid_done")
        split_done = sem2("split_done")
        mhigh_done, mmid_done, msplit_done = sem2("mhigh_done"), sem2("mmid_done"), sem2("msplit_done")
        bst1_done, mvimg_done = sem("bst1_done"), sem("mvimg_done")
        sq_done, e_done = sem("sq_done"), sem("e_done")
        rstdimg_done = sem("rstdimg_done")
        eps_added, epsy_added = sem2("eps_added"), sem("epsy_added")
        xw_done, xl_done = sem("xw_done"), sem("xl_done")
        rden_done = sem2("rden_done")
        h1_done, h1_kept = sem("h1_done"), sem("h1_kept")
        bst_done, mv_done, rstd_done = sem2("bst_done"), sem2("mv_done"), sem2("rstd_done")
        xn_done = sem2("xn_done")
        h2b_done = sem("h2b_done")
        bsty_done, mvy_done = sem("bsty_done"), sem("mvy_done")
        rstdy_done, yn_done, yg_done = sem("rstdy_done"), sem("yn_done"), sem("yg_done")
        res_done = sem("res_done")

        def tiles():
            return [(2 * b + T, b, T, ROWS[T]) for b in range(IMGS) for T in range(2)]

        block = ctx.enter_context(nc.Block())

        @block.sync
        def _(sp):
            sp.dma_start(const[:, :], consts).then_inc(const_in, 16)

            def load_x(u):
                sp.dma_start(xin[:].rearrange("p b c s -> p (b c s)"),
                             x[u].rearrange("p b c s -> p (b c s)") if isinstance(u, int)
                             else x[bass.ds(u, 1)].rearrange("o p b c s -> (o p) (b c s)")
                             ).then_inc(x_in, 16)

            def spill_parts(s, u):
                for g in range(3):
                    sp.wait_ge(split_done[s], 3 * u + g + 1)
                    if g < 2:
                        pieces = [(scratch[s][g], 0, P, 0, HG)]
                    else:
                        pieces = [(scratch[s][0], 0, DB, HG, HEADS), (scratch[s][1], DB, P, HG, HEADS)]
                    for dram, p0, p1, h0, h1_ in pieces:
                        sp.dma_start(dram.rearrange("(e h) a w -> e h (a w)", h=HEADS)[:, h0:h1_, :],
                                     parts[s][p0:p1, g, :, :].rearrange("p a w -> p (a w)")
                                     ).then_inc(parts_out[s], 16)

            def load_stacks(s, u, core):
                sp.wait_ge(parts_out[s], 64 * (u + 1))
                if core is not None:
                    sp.wait_ge(exp_done, STEPS * (core + 1))
                for o, stack, slots in ((0, stack_q[s], SLOT_Q), (1, stack_k[s], SLOT_K)):
                    src = scratch[s][o].rearrange("(e h) a w -> e h a w", h=HEADS)
                    for j, part in enumerate(slots):
                        sp.dma_start(stack[DH * j:DH * (j + 1), :, :], src[:, :, part, :]
                                     ).then_inc(stack_in[s], 16)

            def max_rows(s, u):
                sp.wait_ge(msplit_done[s], u + 1)
                sp.dma_start(scratch_max[s].rearrange("a h w -> h a w"), mparts[s][:]
                             ).then_inc(mparts_out[s], 16)
                sp.wait_ge(mparts_out[s], 16 * (u + 1))
                sp.dma_start(stack_q[s][KS:KM, :, :], scratch_max[s]).then_inc(mrows_in[s], 16)

            def body(B):
                i = B.i
                if B.a:
                    load_x(i + 1)
                if B.c2:
                    max_rows(1, i - 1)
                if B.c1:
                    spill_parts(1, i)
                if B.a:
                    spill_parts(0, i + 1)
                    load_stacks(0, i + 1, B.cores if B.c1 else None)
                if B.a:
                    max_rows(0, i + 1)
                if B.c1:
                    load_stacks(1, i, B.cores + 1 if B.c2 else None)
                if B.c2:
                    u = i - 1
                    sp.wait_ge(res_done, IMGS * (u + 1))
                    for T in range(2):
                        dst = (out[u] if isinstance(u, int)
                               else out[bass.ds(u, 1)].rearrange("o b s d -> (o b) s d"))
                        sp.dma_start(dst[:, COLS[T], :].rearrange("b s d -> s b d"),
                                     res[0:ROWS[T], T::2, :]).then_inc(stored, 16)

            pipeline(nc.sync, units, body)
            sp.wait_ge(stored, 32 * units)

        @block.gpsimd
        def _(pool):
            pool.wait_ge(const_in, 16)
            nc.gpsimd.tensor_tensor(pos_bias[:], c("pos", 2), c("tokb", 2), ALU.add).then_inc(set_up, 1)

            def split(B, s, u, groups):
                for g in groups:
                    k, count = B.job(f"g{s + 1}_{g}")
                    if g == 0 and above(64 * u):
                        pool.wait_ge(parts_out[s], 64 * u)
                    pool.wait_ge(read[k], count)
                    nc.gpsimd.tensor_tensor(parts[s][:, g, 1, :], rest[s][:, g, :],
                                            ones[:].broadcast_to((P, W)),
                                            ALU.mult).then_inc(mid_done[s], 1)
                    pool.wait_ge(mid_done[s], 3 * u + g + 1)
                    nc.gpsimd.tensor_tensor(parts[s][:, g, 2, :], rest[s][:, g, :], parts[s][:, g, 1, :],
                                            ALU.subtract).then_inc(split_done[s], 1)

            def image(t, b):
                return t[:, 2 * b:2 * b + 2, :]

            def inverse_deviations(u, aggregated, eps_added, done):
                pool.wait_ge(aggregated, NT * (u + 1))
                nc.gpsimd.tensor_tensor(var_eps[:], mv[:, :, 1], eps[:], ALU.add).then_inc(eps_added, 1)
                pool.wait_ge(eps_added, u + 1)
                nc.gpsimd.tensor_tensor(rstd[:], var_eps[:], minus_half[:], ALU.pow).then_inc(done, 1)

            def body(B):
                i = B.i
                if B.c1:
                    inverse_deviations(i, mv_done[0], eps_added[0], rstd_done[0])
                    split(B, 1, i, [0])
                if B.a:
                    k, count = B.job("var")
                    pool.wait_ge(read[k], count)
                    nc.gpsimd.tensor_tensor(rstd_img[:], var_img[:], minus_half[:, 0:IMGS],
                                            ALU.pow).then_inc(rstdimg_done, 1)
                if B.c1:
                    split(B, 1, i, [1, 2])
                if B.a:
                    split(B, 0, i + 1, range(3))
                if B.c2:
                    u = i - 1
                    inverse_deviations(u, mv_done[1], eps_added[1], rstd_done[1])
                    for b in range(IMGS):
                        pool.wait_ge(bst_done[1], NT * u + 2 * b + 2)
                        nc.gpsimd.tensor_tensor(image(h2b, b), image(h2, b),
                                                c("bet").unsqueeze(1).broadcast_to((P, 2, D)),
                                                ALU.add).then_inc(h2b_done, 1)
                if B.c1:
                    pool.wait_ge(h1_done, IMGS * (i + 1))
                    nc.gpsimd.tensor_tensor(h1[:], h1_next[:], ones[:].unsqueeze(2).broadcast_to((P, NT, D)),
                                            ALU.mult).then_inc(h1_kept, 1)
                if B.c2:
                    inverse_deviations(u, mvy_done, epsy_added, rstdy_done)
                    for b in range(IMGS):
                        pool.wait_ge(yn_done, NT * u + 2 * b + 2)
                        nc.gpsimd.tensor_tensor(image(yg, b), image(yn, b),
                                                c("gam").unsqueeze(1).broadcast_to((P, 2, D)),
                                                ALU.mult).then_inc(yg_done, 1)
                    if above(32 * u):
                        pool.wait_ge(stored, 32 * u)
                    for b in range(IMGS):
                        pool.wait_ge(yg_done, IMGS * u + b + 1)
                        nc.gpsimd.tensor_tensor(image(res, b), image(yg, b), image(h2b, b),
                                                ALU.add).then_inc(res_done, 1)

            pipeline(nc.gpsimd, units, body)

        @block.scalar
        def _(act):
            act.wait_ge(const_in, 16)

            def exponentials(number):
                for q in range(QUADS):
                    if above(QUADS * number + q - 1):
                        act.wait_ge(av_full, QUADS * number + q - 1)
                    for j in range(4):
                        hp, T = j // 2, j % 2
                        step = 4 * q + j
                        act.wait_ge(sc_full, STEPS * number + step + 1)
                        nc.scalar.activation(
                            probs[0:ROWS[T], q % 2, T, 2 * hp:2 * hp + 2, :],
                            sc_bank[step % 2][0:ROWS[T], 0:2 * S].rearrange("p (h s) -> p h s", h=2),
                            ACT.Exp, scale=float(DH) ** -0.5).then_inc(exp_done, 1)

            def high_parts(B, s, u):
                if above(64 * u):
                    act.wait_ge(parts_out[s], 64 * u)
                for g in range(3):
                    k, n = B.job(f"g{s + 1}_{g}")
                    act.wait_ge(full[k], n)
                    nc.scalar.activation(parts[s][:, g, 0, :], work[k][:, 0:W], ACT.Identity,
                                         bias=group_b[s][:, g:g + 1]).then_inc(high_done[s], 1)

            def high_max(B, s, u):
                if above(16 * u):
                    act.wait_ge(mparts_out[s], 16 * u)
                k, n = B.job(f"mt{s + 1}")
                act.wait_ge(full[k], n)
                nc.scalar.mul(mparts[s][:, 0, :], work[k][0:HEADS, 0:W], -1.0).then_inc(mhigh_done[s], 1)

            def values(B, s):
                for b in range(IMGS):
                    k, n = B.job(f"v{s + 1}_{b}")
                    act.wait_ge(full[k], n)
                    for T in range(2):
                        R = ROWS[T]
                        last = nc.scalar.copy(
                            val[s][0:R, 2 * b + T, :, 0:DH],
                            work[k][0:R, T * D:(T + 1) * D].rearrange("p (h d) -> p h d", h=HEADS))
                    last.then_inc(read[k], 1)

            def evacuate(B, name, dst):
                k, n = B.job(name)
                act.wait_ge(full[k], n)
                nc.scalar.copy(dst[:].rearrange("p b s -> p (b s)"), work[k][:, 0:W]).then_inc(read[k], 1)

            def body(B):
                i = B.i
                if B.c1:
                    exponentials(B.cores)
                if B.c2:
                    high_max(B, 1, i - 1)
                if B.c1:
                    evacuate(B, "xt2_0", xT[1][0])
                    high_parts(B, 1, i)
                if B.a:
                    evacuate(B, "xt1_0", xT[0][0])
                    high_parts(B, 0, i + 1)
                    values(B, 0)
                if B.c2:
                    exponentials(B.cores + int(B.c1))
                if B.a:
                    high_max(B, 0, i + 1)
                if B.c1:
                    values(B, 1)
                if B.c2:
                    evacuate(B, "at_0", aT[0])
                    evacuate(B, "ft_0", fT[0])
                    k, n = B.job("up")
                    act.wait_ge(full[k], n)
                    nc.scalar.activation(hid[:].rearrange("p b s -> p (b s)"), work[k][:, 0:W],
                                         ACT.Relu).then_inc(read[k], 1)

            pipeline(nc.scalar, units, body)

        @block.vector
        def _(dve):
            for s in range(2):
                nc.vector.memset(stack_k[s][KS:KM, :, :], 1.0)
                nc.vector.memset(val[s][:, :, :, DH:2 * DH], 1.0)
            for t in (xT[0][1], xT[1][1], aT[1], fT[1]):
                nc.vector.memset(t[DB:P, :, :], 0.0)
            for t in (mv_img, mv, tok, att, h2, yn):
                nc.vector.memset(t[:], 0.0)
            nc.vector.memset(eps[:], LN_EPS)
            nc.vector.memset(ones[:], 1.0)
            nc.vector.memset(minus_half[:], -0.5).then_inc(zeroed, 1)
            dve.wait_ge(zeroed, 1)
            for t in (xT[0][1], xT[1][1], aT[1], fT[1]):
                last = nc.vector.memset(t[DB:DB + 1, :, :], 1.0)
            last.then_inc(zeroed, 1)
            dve.wait_ge(const_in, 16)
            dve.wait_ge(set_up, 1)
            dve.wait_ge(fold_full, 2)
            nc.vector.tensor_copy(down_w[:], work[0][:, 0:D])
            nc.vector.tensor_copy(down_b[:], work[1][:, 0:D]).then_inc(fold_read, 1)
            dve.wait_ge(fold_read, 1)

            def core(number, passes):
                for q in range(QUADS + 1):
                    if passes is not None and q < QUADS:
                        b, quad = divmod(q, QUADS // IMGS)
                        for j in range(4):
                            hp, T = j // 2, j % 2
                            step, h = 4 * q + j, 4 * quad + 2 * hp
                            dve.wait_ge(mx_full, STEPS * passes + step + 1)
                            nc.vector.tensor_reduce(
                                maxes[0:ROWS[T], 2 * b + T, h:h + 2],
                                mx_bank[step % 2][0:ROWS[T], 0:2 * S].rearrange("p (h s) -> p h s", h=2),
                                AX.X, ALU.max).then_inc(mx_read, 1)
                    if number is not None and q > 0:
                        dve.wait_ge(av_full, QUADS * number + q)
                        nc.vector.tensor_copy(attT[:, q - 1, :], av_bank[:, 0:S]).then_inc(av_read, 1)

            def normalise(B, s, u):
                def divide(n, R):
                    k, count = B.job(f"ot{s + 1}_{n}")
                    dve.wait_ge(rden_done[s], NT * u + n + 1)
                    nc.vector.tensor_tensor(
                        att[0:R, n, :].rearrange("p (h d) -> p h d", h=HEADS),
                        work[k][0:R, 0:2 * D].rearrange("p (h d) -> p h d", h=HEADS)[:, :, 0:DH],
                        rden[0:R, n, :].unsqueeze(2).broadcast_to((R, HEADS, DH)),
                        ALU.mult).then_inc(read[k], 1)

                for n, b, T, R in tiles():
                    k, count = B.job(f"ot{s + 1}_{n}")
                    dve.wait_ge(full[k], count)
                    nc.vector.reciprocal(
                        rden[0:R, n, :],
                        work[k][0:R, 0:2 * D].rearrange("p (h d) -> p h d", h=HEADS)[:, :, DH]
                    ).then_inc(rden_done[s], 1)
                    if n > 0:
                        divide(n - 1, ROWS[(n - 1) % 2])
                divide(NT - 1, ROWS[1])

            def max_rest(B, s, u):
                k, n = B.job(f"mt{s + 1}")
                dve.wait_ge(mhigh_done[s], u + 1)
                nc.vector.scalar_tensor_tensor(mrest[s][:], work[k][0:HEADS, 0:W], -1.0,
                                               mparts[s][:, 0, :], ALU.mult, ALU.subtract
                                               ).then_inc(read[k], 1)
                dve.wait_ge(read[k], n)
                nc.vector.tensor_copy(mparts[s][:, 1, :], mrest[s][:]).then_inc(mmid_done[s], 1)
                dve.wait_ge(mmid_done[s], u + 1)
                nc.vector.tensor_tensor(mparts[s][:, 2, :], mrest[s][:], mparts[s][:, 1, :],
                                        ALU.subtract).then_inc(msplit_done[s], 1)

            def rests(B, s, u, groups):
                if above(3 * u):
                    dve.wait_ge(split_done[s], 3 * u)
                for g in groups:
                    k, n = B.job(f"g{s + 1}_{g}")
                    dve.wait_ge(high_done[s], 3 * u + g + 1)
                    nc.vector.scalar_tensor_tensor(rest[s][:, g, :], work[k][:, 0:W],
                                                   group_b[s][:, g:g + 1], parts[s][:, g, 0, :],
                                                   ALU.add, ALU.subtract).then_inc(read[k], 1)

            def evacuate(B, name, dst):
                k, n = B.job(name)
                dve.wait_ge(full[k], n)
                nc.vector.tensor_copy(dst[0:DB, :, :].rearrange("p b s -> p (b s)"),
                                      work[k][0:DB, 0:W]).then_inc(read[k], 1)

            def wait_for_statistics(stats, u):
                dve.wait_ge(stats, NT * (u + 1))
                nc.vector.memset(spare[:], 0.0)

            def row_norm(src, dst, u, stats, aggregated, inverse, done, src_done):
                for n, b, T, R in tiles():
                    src_done(n)
                    nc.vector.bn_stats(bst[0:R, n, :], src[0:R, n, :]).then_inc(stats, 1)
                wait_for_statistics(stats, u)
                for n, b, T, R in tiles():
                    nc.vector.bn_aggr(mv[0:R, n, :], bst[0:R, n, :]).then_inc(aggregated, 1)
                dve.wait_ge(inverse, u + 1)
                for n, b, T, R in tiles():
                    nc.vector.tensor_scalar(dst[0:R, n, :], src[0:R, n, :], mv[0:R, n, 0:1],
                                            rstd[0:R, n:n + 1], ALU.subtract, ALU.mult).then_inc(done, 1)

            def body(B):
                i = B.i
                if B.c1 or B.c2:
                    core(B.cores if B.c1 else None, B.passes if B.c2 else None)
                if B.c1:
                    normalise(B, 0, i)
                    if above(i):
                        dve.wait_ge(h1_kept, i)
                    for b in range(IMGS):
                        for n in (2 * b, 2 * b + 1):
                            k, count = B.job(f"ot1_{n}")
                            dve.wait_ge(read[k], count)
                        nc.vector.tensor_tensor(h1_next[:, 2 * b:2 * b + 2, :], att[:, 2 * b:2 * b + 2, :],
                                                tok[:, 2 * b:2 * b + 2, :], ALU.add).then_inc(h1_done, 1)
                if B.c2:
                    max_rest(B, 1, i - 1)
                if B.c1:
                    row_norm(h1_next, xn, i, bst_done[0], mv_done[0], rstd_done[0], xn_done[0],
                             lambda n: dve.wait_ge(h1_done, IMGS * i + n // 2 + 1))
                if B.a:
                    u = i + 1
                    for b in range(IMGS):
                        k, count = B.job(f"emb_{b}")
                        dve.wait_ge(full[k], count)
                        for T in range(2):
                            R = ROWS[T]
                            last = nc.vector.tensor_tensor(tok[0:R, 2 * b + T, :],
                                                           work[k][0:R, T * D:(T + 1) * D],
                                                           pos_bias[0:R, T, :], ALU.add)
                        last.then_inc(read[k], 1)
                    for n, b, T, R in tiles():
                        k, count = B.job(f"emb_{b}")
                        dve.wait_ge(read[k], count)
                        nc.vector.bn_stats(bst1[0:R, n, :], tok[0:R, n, :]).then_inc(bst1_done, 1)
                    wait_for_statistics(bst1_done, u)
                    for n, b, T, R in tiles():
                        nc.vector.bn_aggr(mv_img[0:R, T, b, :], bst1[0:R, n, :]).then_inc(mvimg_done, 1)
                if B.c1:
                    evacuate(B, "xt2_1", xT[1][1])
                if B.a:
                    k, count = B.job("mean")
                    dve.wait_ge(full[k], count)
                    nc.vector.tensor_copy(mean_img[:], work[k][:, 0:IMGS])
                    nc.vector.tensor_tensor(dev_img[:], mv_img[:, :, :, 0],
                                            work[k][:, 0:IMGS].unsqueeze(1).broadcast_to((P, 2, IMGS)),
                                            ALU.subtract).then_inc(read[k], 1)
                    dve.wait_ge(read[k], count)
                    nc.vector.tensor_tensor(sq_img[:], dev_img[:], dev_img[:], ALU.mult).then_inc(sq_done, 1)
                    dve.wait_ge(sq_done, u + 1)
                    nc.vector.tensor_tensor(e_img[:], sq_img[:], mv_img[:, :, :, 1],
                                            ALU.add).then_inc(e_done, 1)
                if B.c1:
                    rests(B, 1, i, [0])
                if B.a:
                    k, count = B.job("var")
                    dve.wait_ge(full[k], count)
                    nc.vector.tensor_scalar(var_img[:], work[k][:, 0:IMGS], LN_EPS, None,
                                            ALU.add).then_inc(read[k], 1)
                if B.c1:
                    rests(B, 1, i, [1, 2])
                if B.a:
                    for n, b, T, R in tiles():
                        nc.vector.scalar_tensor_tensor(xw[0:R, n, :], tok[0:R, n, :],
                                                       mean_img[0:R, b:b + 1], lnw[0:R, T, :],
                                                       ALU.subtract, ALU.mult).then_inc(xw_done, 1)
                    dve.wait_ge(rstdimg_done, u + 1)
                    for n, b, T, R in tiles():
                        dve.wait_ge(xw_done, NT * u + n + 1)
                        nc.vector.scalar_tensor_tensor(xl[0:R, n, :], xw[0:R, n, :],
                                                       rstd_img[0:R, b:b + 1], lnb[0:R, T, :],
                                                       ALU.mult, ALU.add).then_inc(xl_done, 1)
                    evacuate(B, "xt1_1", xT[0][1])
                    rests(B, 0, u, range(3))
                if B.c2 or B.a:
                    core(B.cores + int(B.c1) if B.c2 else None, B.passes + int(B.c2) if B.a else None)
                if B.c2:
                    normalise(B, 1, i - 1)
                if B.a:
                    max_rest(B, 0, i + 1)
                if B.c2:
                    u = i - 1
                    evacuate(B, "at_1", aT[1])
                    if above(IMGS * u):
                        dve.wait_ge(h2b_done, IMGS * u)
                    for b in range(IMGS):
                        k, count = B.job(f"proj_{b}")
                        dve.wait_ge(full[k], count)
                        for T in range(2):
                            R = ROWS[T]
                            if b == 0 and T == 0:
                                dve.wait_ge(h1_kept, u + 1)
                            last = nc.vector.tensor_tensor(h2[0:R, 2 * b + T, :],
                                                           work[k][0:R, T * D:(T + 1) * D],
                                                           h1[0:R, 2 * b + T, :], ALU.add)
                        last.then_inc(read[k], 1)
                    row_norm(h2, xn, u, bst_done[1], mv_done[1], rstd_done[1], xn_done[1],
                             lambda n: dve.wait_ge(read[B.job(f"proj_{n // 2}")[0]], B.job(f"proj_{n // 2}")[1]))
                    evacuate(B, "ft_1", fT[1])
                    for b in range(IMGS):
                        k, count = B.job(f"down_{b}")
                        dve.wait_ge(full[k], count)
                        for T in range(2):
                            R = ROWS[T]
                            last = nc.vector.tensor_tensor(y[0:R, 2 * b + T, :],
                                                           work[k][0:R, T * D:(T + 1) * D],
                                                           down_b[0:R, :], ALU.add)
                        last.then_inc(read[k], 1)
                    if above(IMGS * u):
                        dve.wait_ge(yg_done, IMGS * u)
                    row_norm(y, yn, u, bsty_done, mvy_done, rstdy_done, yn_done,
                             lambda n: dve.wait_ge(read[B.job(f"down_{n // 2}")[0]], B.job(f"down_{n // 2}")[1]))

            pipeline(nc.vector, units, body)

        @block.tensor
        def _(pe):
            pe.wait_ge(const_in, 16)
            pe.wait_ge(zeroed, 2)

            for k, (name, n) in enumerate((("w2", INNER), ("b2", P))):
                for half in range(2):
                    last = nc.tensor.matmul(work[k][:, 0:D], c(name, 2)[:, half, :], c("wo", 2)[:, half, :],
                                            start=half == 0, stop=half == 1)
                last.then_inc(fold_full, 1)
            pe.wait_ge(fold_read, 1)

            def begin(B, name):
                k, n = B.job(name)
                if above(n - 1):
                    pe.wait_ge(read[k], n - 1)
                return k, work[k]

            def was_read(B, name):
                k, n = B.job(name)
                pe.wait_ge(read[k], n)

            def step_of(step):
                q, j = divmod(step, 4)
                b, quad = divmod(q, QUADS // IMGS)
                return b, 4 * quad + 2 * (j // 2), j % 2

            def part(stack, rows, h, b, cols):
                return stack[0:rows, h, b * S + cols.start:b * S + cols.stop]

            def core(scores, maxima):
                for q in range(QUADS):
                    for j in range(4):
                        step = 4 * q + j
                        b, h0, T = step_of(step)
                        if maxima is not None:
                            s, u, number = maxima
                            if step == 0:
                                pe.wait_ge(stack_in[s], 192 * (u + 1))
                            if above(STEPS * number + step - 1):
                                pe.wait_ge(mx_read, STEPS * number + step - 1)
                            for h in (0, 1):
                                last = nc.tensor.matmul(
                                    mx_bank[step % 2][0:ROWS[T], h * S:(h + 1) * S],
                                    part(stack_q[s], KS, h0 + h, b, COLS[T]),
                                    part(stack_k[s], KS, h0 + h, b, slice(0, S)), start=True, stop=True)
                            last.then_inc(mx_full, 1)
                        if scores is not None:
                            s, u, number = scores
                            if step == 0:
                                pe.wait_ge(mrows_in[s], 16 * (u + 1))
                            if above(STEPS * number + step - 1):
                                pe.wait_ge(exp_done, STEPS * number + step - 1)
                            for h in (0, 1):
                                last = nc.tensor.matmul(
                                    sc_bank[step % 2][0:ROWS[T], h * S:(h + 1) * S],
                                    part(stack_k[s], KM, h0 + h, b, COLS[T]),
                                    part(stack_q[s], KM, h0 + h, b, slice(0, S)), start=True, stop=True)
                            last.then_inc(sc_full, 1)
                    if scores is not None and q > 0:
                        times_values(scores, q - 1)
                if scores is not None:
                    times_values(scores, QUADS - 1)

            def times_values(scores, q):
                s, u, number = scores
                b, quad = divmod(q, QUADS // IMGS)
                pe.wait_ge(exp_done, STEPS * number + 4 * (q + 1))
                if above(QUADS * number + q):
                    pe.wait_ge(av_read, QUADS * number + q)
                for T in range(2):
                    R = ROWS[T]
                    for h in range(4):
                        last = nc.tensor.matmul(av_bank[2 * DH * h:2 * DH * (h + 1), 0:S],
                                                val[s][0:R, 2 * b + T, 4 * quad + h, :],
                                                probs[0:R, q % 2, T, h, :], start=T == 0, stop=T == 1)
                last.then_inc(av_full, 1)

            def attention_rows(B, s, number):
                for n, b, T, R in tiles():
                    k, ps = begin(B, f"ot{s + 1}_{n}")
                    pe.wait_ge(av_read, QUADS * number + 3 * (b + 1))
                    for quad in range(3):
                        last = nc.tensor.transpose(ps[0:R, quad * P:(quad + 1) * P],
                                                   attT[:, 3 * b + quad, COLS[T]], ident)
                    last.then_inc(full[k], 1)

            def max_columns(B, s, passes):
                k, ps = begin(B, f"mt{s + 1}")
                pe.wait_ge(mx_read, STEPS * (passes + 1))
                for n, b, T, R in tiles():
                    last = nc.tensor.transpose(ps[0:HEADS, b * S + COLS[T].start:b * S + COLS[T].stop],
                                               maxes[0:R, n, :], ident[0:R, 0:R])
                last.then_inc(full[k], 1)

            def transposed(B, name, src, src_done):
                banks = [begin(B, f"{name}_{half}") for half in range(2)]
                for half, (k, ps) in enumerate(banks):
                    for n, b, T, R in tiles():
                        if half == 0:
                            src_done(n)
                        width = (P, DB)[half]
                        last = nc.tensor.transpose(ps[0:width, b * S + COLS[T].start:b * S + COLS[T].stop],
                                                   src[0:R, n, half * P:half * P + width],
                                                   ident[0:R, 0:R])
                    last.then_inc(full[k], 1)

            def groups(B, s, which):
                for g in which:
                    k, ps = begin(B, f"g{s + 1}_{g}")
                    halves = ([1] if g == 2 else [0]) if s == 0 else [0, 1]
                    for half in halves:
                        last = nc.tensor.matmul(ps[:, 0:W], group_w[s][:, half, g * P:(g + 1) * P],
                                                xT[s][half][:].rearrange("p b s -> p (b s)"),
                                                start=half == halves[0], stop=half == halves[-1])
                    last.then_inc(full[k], 1)

            def rows_times(B, name, xT_, w):
                for b in range(IMGS):
                    k, ps = begin(B, f"{name}_{b}")
                    for T in range(2):
                        for half in range(len(xT_)):
                            last = nc.tensor.matmul(ps[0:ROWS[T], T * D:(T + 1) * D],
                                                    xT_[half][:, b, COLS[T]], w[half],
                                                    start=half == 0, stop=half == len(xT_) - 1)
                    last.then_inc(full[k], 1)

            def image_sum(B, name, rhs):
                k, ps = begin(B, name)
                for T in range(2):
                    last = nc.tensor.matmul(ps[:, 0:IMGS], avg[0:ROWS[T], :], rhs(T),
                                            start=T == 0, stop=T == 1)
                last.then_inc(full[k], 1)

            def body(B):
                i = B.i
                if B.c1 or B.c2:
                    core((0, i, B.cores) if B.c1 else None, (1, i - 1, B.passes) if B.c2 else None)
                if B.c1:
                    attention_rows(B, 0, B.cores)
                if B.c2:
                    max_columns(B, 1, B.passes)
                if B.a:
                    u = i + 1
                    pe.wait_ge(x_in, 16 * (u + 1))
                    for b in range(IMGS):
                        k, ps = begin(B, f"emb_{b}")
                        for T in range(2):
                            for ch in range(CH):
                                last = nc.tensor.matmul(ps[0:ROWS[T], T * D:(T + 1) * D],
                                                        xin[:, b, ch, COLS[T]], wm[:, ch, :],
                                                        start=ch == 0, stop=ch == CH - 1)
                        last.then_inc(full[k], 1)
                if B.c1:
                    transposed(B, "xt2", xn, lambda n: pe.wait_ge(xn_done[0], NT * i + n + 1))
                if B.a:
                    pe.wait_ge(mvimg_done, NT * (u + 1))
                    image_sum(B, "mean", lambda T: mv_img[0:ROWS[T], T, :, 0])
                if B.c1:
                    was_read(B, "xt2_0")
                    was_read(B, "xt2_1")
                    groups(B, 1, [0])
                if B.a:
                    pe.wait_ge(e_done, u + 1)
                    image_sum(B, "var", lambda T: e_img[0:ROWS[T], T, :])
                if B.c1:
                    groups(B, 1, [1, 2])
                if B.a:
                    transposed(B, "xt1", xl, lambda n: pe.wait_ge(xl_done, NT * u + n + 1))
                    was_read(B, "xt1_0")
                    was_read(B, "xt1_1")
                    groups(B, 0, range(3))
                    rows_times(B, "v1", xT[0], [value_w[0][:, 0, :], value_w[0][:, 1, :]])
                if B.c2 or B.a:
                    core((1, i - 1, B.cores + int(B.c1)) if B.c2 else None,
                         (0, i + 1, B.passes + int(B.c2)) if B.a else None)
                if B.c2:
                    attention_rows(B, 1, B.cores + int(B.c1))
                if B.a:
                    max_columns(B, 0, B.passes + int(B.c2))
                if B.c1:
                    rows_times(B, "v2", xT[1], [value_w[1][:, 0, :], value_w[1][:, 1, :]])
                if B.c2:
                    u = i - 1
                    transposed(B, "at", att, lambda n: was_read(B, f"ot2_{n}"))
                    was_read(B, "at_0")
                    was_read(B, "at_1")
                    rows_times(B, "proj", aT, [proj_w[:, 0, :], proj_w[:, 1, :]])
                    transposed(B, "ft", xn, lambda n: pe.wait_ge(xn_done[1], NT * u + n + 1))
                    was_read(B, "ft_0")
                    was_read(B, "ft_1")
                    k, ps = begin(B, "up")
                    for half in range(2):
                        last = nc.tensor.matmul(ps[:, 0:W], up_w[:, half, :],
                                                fT[half][:].rearrange("p b s -> p (b s)"),
                                                start=half == 0, stop=half == 1)
                    last.then_inc(full[k], 1)
                    was_read(B, "up")
                    rows_times(B, "down", [hid], [down_w[:]])

            pipeline(nc.tensor, units, body)


def kernel(x, L0_tok_W_map, L0_tok_b_map, L0_tok_class_token, L0_tok_ln_w, L0_tok_ln_b, L0_tok_Wq,
           L0_tok_bq, L0_tok_Wk, L0_tok_bk, L0_tok_Wv, L0_tok_bv, L0_attn_w_attn, L0_attn_b_attn,
           L0_attn_w_proj, L0_attn_b_proj, L0_ffn_W1, L0_ffn_b1, L0_ffn_W2, L0_ffn_b2, L0_ffn_Wo,
           L0_ffn_bo, L0_ffn_gamma, L0_ffn_beta):
    import numpy as np
    import concourse.bacc as bacc
    from concourse.bass_utils import run_bass_kernel_spmd

    f32 = np.float32
    images = np.asarray(x)
    units = images.shape[0] // IMGS

    patches = images.reshape(units, IMGS, S - 1, CH, P)
    x_host = np.zeros((units, P, IMGS, CH, S), f32)
    x_host[..., 1:] = patches.transpose(0, 4, 1, 3, 2)

    packed = np.zeros((P, NCONST), f32)

    def put(name, value):
        at, n = CONST[name]
        value = np.asarray(value)
        chunks = value[None] if value.ndim == 2 else value
        per = n // len(chunks)
        for k, v in enumerate(chunks):
            packed[:v.shape[0], at + k * per:at + k * per + v.shape[1]] = v

    def row_tiles(a):
        t = np.zeros((2, P, D), f32)
        t[0], t[1, :S - P] = a[:P], a[P:]
        return t

    def contraction(a, bias=None):
        t = np.zeros((2, P, a.shape[1]), f32)
        t[0], t[1, :DB] = a[:P], a[P:]
        if bias is not None:
            t[1, DB] = bias
        return t

    def blocks(w):
        t = np.zeros((D, D), f32)
        for h in range(HEADS):
            t[h * DH:(h + 1) * DH, h * DH:(h + 1) * DH] = w[h].T
        return t

    def grouped(q, k):
        def heads(a, h0, h1):
            a = a.reshape(a.shape[:-1] + (HEADS, DH))[..., h0:h1, :]
            return np.swapaxes(a, -1, -2).reshape(a.shape[:-2] + (-1,))
        return np.concatenate([heads(q, 0, HG), heads(k, 0, HG), heads(q, HG, HEADS),
                               heads(k, HG, HEADS)], axis=-1)

    i = np.arange(S, dtype=f32)[:, None]
    j = np.arange(D, dtype=f32)[None, :]
    pos = np.where((np.arange(D) % 2 == 0)[None, :], np.sin(i / np.power(f32(10000.0), j / f32(D))),
                   np.cos(i / np.power(f32(10000.0), (j - f32(1.0)) / f32(D)))).astype(f32)
    tokb = np.zeros((S, D), f32)
    tokb[0], tokb[1:] = np.asarray(L0_tok_class_token)[0], np.asarray(L0_tok_b_map)

    wq, wk, wv = (blocks(np.asarray(w)) for w in (L0_tok_Wq, L0_tok_Wk, L0_tok_Wv))
    w_attn, b_attn = np.asarray(L0_attn_w_attn), np.asarray(L0_attn_b_attn)

    put("wm", np.asarray(L0_tok_W_map).T.reshape(CH, P, D))
    put("pos", row_tiles(pos))
    put("tokb", row_tiles(tokb))
    put("lnw", row_tiles(np.asarray(L0_tok_ln_w)))
    put("lnb", row_tiles(np.asarray(L0_tok_ln_b)))
    put("g1", contraction(grouped(wq, wk)))
    put("g2", contraction(grouped(w_attn[:, :D], w_attn[:, D:2 * D])))
    put("gb1", grouped(np.asarray(L0_tok_bq).reshape(D), np.asarray(L0_tok_bk).reshape(D)).reshape(3, P).T)
    put("gb2", grouped(b_attn[:D], b_attn[D:2 * D]).reshape(3, P).T)
    put("wv1", contraction(wv, np.asarray(L0_tok_bv).reshape(D)))
    put("wv2", contraction(w_attn[:, 2 * D:], b_attn[2 * D:]))
    put("wp", contraction(np.asarray(L0_attn_w_proj), np.asarray(L0_attn_b_proj)))
    put("w1", contraction(np.asarray(L0_ffn_W1).T, np.asarray(L0_ffn_b1)))
    put("w2", contraction(np.asarray(L0_ffn_W2)))
    put("wo", contraction(np.asarray(L0_ffn_Wo).T, np.asarray(L0_ffn_bo)))
    put("b2", contraction(np.broadcast_to(np.asarray(L0_ffn_b2)[:, None], (D, P)), np.ones(P, f32)))
    put("gam", np.broadcast_to(np.asarray(L0_ffn_gamma), (P, D)))
    put("bet", np.broadcast_to(np.asarray(L0_ffn_beta), (P, D)))
    put("ident", np.eye(P, dtype=f32))
    put("avg", np.full((P, P), 1.0 / S, f32))

    nc = bacc.Bacc("TRN2", target_bir_lowering=False, num_devices=1)
    x_dram = nc.dram_tensor("x_dram", x_host.shape, F32, kind="ExternalInput").ap()
    const_dram = nc.dram_tensor("const_dram", packed.shape, F32, kind="ExternalInput").ap()
    out_dram = nc.dram_tensor("out_dram", (units, IMGS, S, D), F32, kind="ExternalOutput").ap()
    vit_tower(nc, x_dram, const_dram, out_dram)
    result = run_bass_kernel_spmd(nc, [{"x_dram": x_host, "const_dram": packed}], core_ids=[0])
    return result.results[0]["out_dram"].reshape(images.shape[0], S, D)
```

```python
from contextlib import ExitStack

import concourse.bass as bass
from concourse import mybir

F32 = mybir.dt.float32
BF16 = mybir.dt.bfloat16
ALU = mybir.AluOpType
ACT = mybir.ActivationFunctionType
AX = mybir.AxisListType

P = 128
IMGS = 2
S = 197
D = 192
HEADS = 12
DH = D // HEADS
DB = D - P
PIX = 768
CH = PIX // P
INNER = 128
LN_EPS = 1e-5
ROWS = [P, S - P]
COLS = [slice(0, P), slice(P, S)]
NT = 2 * IMGS
W = IMGS * S
PARTS = 3
SLOT_Q = [0, 0, 0, 1, 1, 2]
SLOT_K = [0, 1, 2, 0, 1, 0]
KS = len(SLOT_Q) * DH
KM = KS + PARTS
QUADS = IMGS * HEADS // 4
STEPS = 4 * QUADS
HG = 8

_SIZES = [("wm", CH * D), ("pos", 2 * D), ("tokb", 2 * D), ("lnw", 2 * D), ("lnb", 2 * D),
          ("g1", 2 * 3 * P), ("g2", 2 * 3 * P), ("gb1", 3), ("gb2", 3), ("wv1", 2 * D),
          ("wv2", 2 * D), ("wp", 2 * D), ("w1", 2 * INNER), ("w2", 2 * INNER), ("wo", 2 * D),
          ("b2", 2 * P), ("gam", D), ("bet", D), ("ident", P), ("avg", P)]
CONST = {}
_at = 0
for _name, _n in _SIZES:
    CONST[_name] = (_at, _n)
    _at += _n
NCONST = _at

JOBS = ([("ot1_0", "c1"), ("ot1_1", "c1"), ("mt2", "c2"), ("ot1_2", "c1"), ("ot1_3", "c1")]
        + [("emb_0", "e"), ("xt2_0", "c1"), ("xt2_1", "c1"), ("emb_1", "e")]
        + [(f"g2_{g}", "c1") for g in range(3)] + [("mean", "e"), ("var", "e"), ("", None)]
        + [("ot2_0", "c2"), ("ot2_1", "c2"), ("mt1", "a"), ("ot2_2", "c2"), ("ot2_3", "c2")]
        + [("v1_0", "a"), ("v1_1", "a"), ("xt1_0", "e"), ("xt1_1", "e"), ("at_0", "c2"), ("at_1", "c2")]
        + [("g1_0", "e"), ("g1_1", "e"), ("proj_0", "c2"), ("proj_1", "c2"), ("g1_2", "e")]
        + [("v2_0", "c1"), ("v2_1", "c1"), ("ft_0", "c2"), ("ft_1", "c2")]
        + [("up", "c2"), ("down_0", "c2"), ("down_1", "c2")])
AHEAD = 2
NBANK = 3
LENT = NBANK - 1
FIRST = 3


class Body:

    def __init__(self, i, units, before, passes, cores, full=False):
        self.i, self.before, self.passes, self.cores = i, before, passes, cores
        self.c1, self.c2, self.c3, self.a, self.e = (full or 0 <= i + k < units
                                                     for k in (0, -1, -2, 1, 2))

    def has(self, unit):
        return {"c1": self.c1, "c2": self.c2, "a": self.a, "e": self.e, None: False}[unit]

    def jobs_per_bank(self):
        n = [0] * NBANK
        for k, (_, unit) in enumerate(JOBS):
            n[k % NBANK] += self.has(unit)
        return n

    def job(self, name):
        done = list(self.before)
        for k, (other, unit) in enumerate(JOBS):
            done[k % NBANK] = done[k % NBANK] + int(self.has(unit))
            if other == name:
                return k % NBANK, done[k % NBANK]
        raise KeyError(name)

    def last(self, name):
        k = [other for other, _ in JOBS].index(name) % NBANK
        return k, self.before[k]

    def lent(self, s):
        stop = JOBS.index((f"ot{s + 1}_0", ("c1", "c2")[s]))
        return self.before[LENT] + sum(self.has(unit) for _, unit in JOBS[LENT:stop:NBANK])

    def after(self, times=1):
        return ([x + times * n for x, n in zip(self.before, self.jobs_per_bank())],
                self.passes + times * (self.c2 + self.a), self.cores + times * (self.c1 + self.c2))


def pipeline(eng, units, emit):
    before = ([0] * NBANK, 0, 0)
    for i in range(-2, FIRST):
        body = Body(i, units, *before)
        emit(body)
        before = body.after()
    loops = units - 2 - FIRST
    full = Body(FIRST, units, *before, full=True)
    with eng.Fori(FIRST, FIRST + loops) as i:
        t = i - FIRST
        emit(Body(i, units, [x + t * m for x, m in zip(before[0], full.jobs_per_bank())],
                  before[1] + t * 2, before[2] + t * 2, full=True))
    before = full.after(loops)
    for i in range(units - 2, units + 2):
        body = Body(i, units, *before)
        emit(body)
        before = body.after()


def above(value):
    return not isinstance(value, int) or value > 0


def vit_tower(nc: bass.Bass, x, consts, out):
    units = x.shape[0]
    scratch = [[nc.dram_tensor(f"parts_{o}{s}", (DH * HEADS, PARTS, W), BF16).ap() for o in "qk"]
               for s in (1, 2)]
    scratch_max = [nc.dram_tensor(f"parts_max{s}", (PARTS, HEADS, W), BF16).ap() for s in (1, 2)]

    with ExitStack() as ctx:
        def sb(name, shape, dt=F32):
            return ctx.enter_context(nc.sbuf_tensor(name, shape, dt))

        def bank(name):
            return ctx.enter_context(nc.psum_tensor(name, [P, 512], F32))

        def sem(name):
            return ctx.enter_context(nc.semaphore(name))

        def sem2(name):
            return [sem(f"{name}{s}") for s in (1, 2)]

        const = sb("const", [P, NCONST])

        def c(name, *split):
            at, n = CONST[name]
            v = const[:, at:at + n]
            return v.rearrange("p (a n) -> p a n", a=split[0]) if split else v

        wm, lnw, lnb = c("wm", CH), c("lnw", 2), c("lnb", 2)
        group_w, group_b = [c("g1", 2), c("g2", 2)], [c("gb1"), c("gb2")]
        value_w, proj_w, up_w = [c("wv1", 2), c("wv2", 2)], c("wp", 2), c("w1", 2)
        ident, avg = c("ident"), c("avg")
        pos_bias = sb("pos_bias", [P, 2, D])
        down_w = sb("down_w", [P, D])
        down_b = sb("down_b", [P, D])

        xin = sb("xin", [P, IMGS, CH, S])
        tok_next = sb("tok_next", [P, NT, D])
        tok = sb("tok", [P, NT, D])
        bst = sb("bst", [P, NT, 6])
        bst1 = sb("bst1", [P, NT, 6])
        mv_img = sb("mv_img", [P, 2, IMGS, 2])
        dev_img = sb("dev_img", [P, 2, IMGS])
        sq_img = sb("sq_img", [P, 2, IMGS])
        e_img = sb("e_img", [P, 2, IMGS])
        mean_img = sb("mean_img", [P, IMGS])
        var_img = sb("var_img", [P, IMGS])
        rstd_img = sb("rstd_img", [P, IMGS])
        xw = sb("xw", [P, NT, D])
        xg = sb("xg", [P, NT, D])
        xl = sb("xl", [P, NT, D])
        xT = [[sb(f"xT{s}{k}", [P, IMGS, S]) for k in "AB"] for s in (1, 2)]
        aT = [sb(f"aT{k}", [P, IMGS, S]) for k in "AB"]
        fT = [sb(f"fT{k}", [P, IMGS, S]) for k in "AB"]
        parts = [sb(f"parts{s}", [P, 3, PARTS, W], BF16) for s in (1, 2)]
        rest = [sb(f"rest{s}", [P, 3, W]) for s in (1, 2)]
        stack_q = [sb(f"stack_q{s}", [KM, HEADS, W], BF16) for s in (1, 2)]
        stack_k = [sb(f"stack_k{s}", [KM, HEADS, W], BF16) for s in (1, 2)]
        maxes = sb("maxes", [P, NT, HEADS])
        mparts = [sb(f"mparts{s}", [HEADS, PARTS, W], BF16) for s in (1, 2)]
        mneg = [sb(f"mneg{s}", [HEADS, W]) for s in (1, 2)]
        mrest = [sb(f"mrest{s}", [HEADS, W]) for s in (1, 2)]
        val = [sb(f"val{s}", [P, NT, HEADS, 2 * DH]) for s in (1, 2)]
        probs = sb("probs", [P, 2, 2, 4, S])
        attT = sb("attT", [P, QUADS, S])
        rden = sb("rden", [P, NT, HEADS])
        att = sb("att", [P, NT, D])
        h1_next = sb("h1_next", [P, NT, D])
        h1 = sb("h1", [P, NT, D])
        mv = sb("mv", [P, NT, 2])
        rstd = sb("rstd", [P, NT])
        var_eps = sb("var_eps", [P, NT])
        spare = sb("spare", [P, 1])
        eps = sb("eps", [P, NT])
        ones = sb("ones", [P, 1])
        minus_half = sb("minus_half", [P, NT])
        xn1 = sb("xn1", [P, NT, D])
        xn2 = sb("xn2", [P, NT, D])
        h2 = sb("h2", [P, NT, D])
        h2b = sb("h2b", [P, NT, D])
        hid = sb("hid", [P, IMGS, S])
        down = sb("down", [P, NT, D])
        y = sb("y", [P, NT, D])
        yn = sb("yn", [P, NT, D])
        yg = sb("yg", [P, NT, D])
        res = sb("res", [P, NT, D])

        mx_bank = [bank("mx_bank0"), bank("mx_bank1")]
        sc_bank = [bank("sc_bank0"), bank("sc_bank1")]
        work = [bank(f"work{k}") for k in range(NBANK)]
        av_bank = [bank("av_bank"), work[LENT]]

        const_in = sem("const_in")
        x_in = sem("x_in")
        parts_out = sem2("parts_out")
        stack_in = sem2("stack_in")
        mparts_out = sem2("mparts_out")
        mrows_in = sem2("mrows_in")
        stored = sem("stored")
        zeroed = sem("zeroed")
        set_up = sem("set_up")
        fold_full = sem("fold_full")
        fold_read = sem("fold_read")
        full = [sem(f"work_full{k}") for k in range(NBANK)]
        read = [sem(f"work_read{k}") for k in range(NBANK)]
        mx_full, mx_read = sem("mx_full"), sem("mx_read")
        sc_full, exp_done = sem("sc_full"), sem("exp_done")
        av_full, av_read = sem("av_full"), sem("av_read")
        high_done = sem2("high_done")
        mid_done = sem2("mid_done")
        split_done = sem2("split_done")
        mrest_done, mmid_done, msplit_done = sem2("mrest_done"), sem2("mmid_done"), sem2("msplit_done")
        bst1_done, mvimg_done = sem("bst1_done"), sem("mvimg_done")
        sq_done, e_done = sem("sq_done"), sem("e_done")
        rstdimg_done = sem("rstdimg_done")
        eps_added, epsy_added = sem2("eps_added"), sem("epsy_added")
        xw_done, xg_done, xl_done = sem("xw_done"), sem("xg_done"), sem("xl_done")
        rden_done = sem2("rden_done")
        tok_kept, h1_done, h1_kept = sem("tok_kept"), sem("h1_done"), sem("h1_kept")
        bst_done, mv_done, rstd_done = sem2("bst_done"), sem2("mv_done"), sem2("rstd_done")
        xn_done = sem2("xn_done")
        h2b_done = sem("h2b_done")
        y_done = sem("y_done")
        bsty_done, mvy_done = sem("bsty_done"), sem("mvy_done")
        rstdy_done, yn_done, yg_done = sem("rstdy_done"), sem("yn_done"), sem("yg_done")
        res_done = sem("res_done")

        def tiles():
            return [(2 * b + T, b, T, ROWS[T]) for b in range(IMGS) for T in range(2)]

        block = ctx.enter_context(nc.Block())

        @block.sync
        def _(sp):
            sp.dma_start(const[:, :], consts).then_inc(const_in, 16)

            def load_x(u):
                sp.dma_start(xin[:].rearrange("p b c s -> p (b c s)"),
                             x[u].rearrange("p b c s -> p (b c s)") if isinstance(u, int)
                             else x[bass.ds(u, 1)].rearrange("o p b c s -> (o p) (b c s)")
                             ).then_inc(x_in, 16)

            def spill_parts(s, u):
                for g in range(3):
                    sp.wait_ge(split_done[s], 3 * u + g + 1)
                    if g < 2:
                        pieces = [(scratch[s][g], 0, P, 0, HG)]
                    else:
                        pieces = [(scratch[s][0], 0, DB, HG, HEADS), (scratch[s][1], DB, P, HG, HEADS)]
                    for dram, p0, p1, h0, h1_ in pieces:
                        sp.dma_start(dram.rearrange("(e h) a w -> e h (a w)", h=HEADS)[:, h0:h1_, :],
                                     parts[s][p0:p1, g, :, :].rearrange("p a w -> p (a w)")
                                     ).then_inc(parts_out[s], 16)

            def load_stack(s, o, stack, slots):
                src = scratch[s][o].rearrange("(e h) a w -> e h a w", h=HEADS)
                for j, part in enumerate(slots):
                    sp.dma_start(stack[DH * j:DH * (j + 1), :, :], src[:, :, part, :]
                                 ).then_inc(stack_in[s], 16)

            def spill_max(s, u):
                sp.wait_ge(msplit_done[s], u + 1)
                sp.dma_start(scratch_max[s].rearrange("a h w -> h a w"), mparts[s][:]
                             ).then_inc(mparts_out[s], 16)

            def load_max(s, u):
                sp.wait_ge(mparts_out[s], 16 * (u + 1))
                sp.dma_start(stack_q[s][KS:KM, :, :], scratch_max[s]).then_inc(mrows_in[s], 16)

            def stacks_and_maxima(load, load_unit, core, rows, rows_unit):
                if load is not None:
                    sp.wait_ge(parts_out[load], 64 * (load_unit + 1))
                    if core is not None:
                        sp.wait_ge(exp_done, STEPS * (core + 1))
                    load_stack(load, 0, stack_q[load], SLOT_Q)
                    load_stack(load, 1, stack_k[load], SLOT_K)
                if rows is not None:
                    spill_max(rows, rows_unit)
                    load_max(rows, rows_unit)

            def body(B):
                i = B.i
                if B.e:
                    load_x(i + 2)
                if B.c3:
                    u = i - 2
                    sp.wait_ge(res_done, IMGS * (u + 1))
                    for T in range(2):
                        dst = (out[u] if isinstance(u, int)
                               else out[bass.ds(u, 1)].rearrange("o b s d -> (o b) s d"))
                        sp.dma_start(dst[:, COLS[T], :].rearrange("b s d -> s b d"),
                                     res[0:ROWS[T], T::2, :]).then_inc(stored, 16)
                stacks_and_maxima(0 if B.a else None, i + 1, B.cores if B.c1 else None,
                                  1 if B.c2 else None, i - 1)
                if B.c1:
                    spill_parts(1, i)
                stacks_and_maxima(1 if B.c1 else None, i, B.cores + int(B.c1) if B.c2 else None,
                                  0 if B.a else None, i + 1)
                if B.e:
                    spill_parts(0, i + 2)
            pipeline(nc.sync, units, body)
            sp.wait_ge(stored, 32 * units)

        @block.gpsimd
        def _(pool):
            pool.wait_ge(const_in, 16)
            pool.wait_ge(fold_read, 1)
            nc.gpsimd.tensor_tensor(pos_bias[:], c("pos", 2), c("tokb", 2), ALU.add).then_inc(set_up, 1)

            def split(B, s, u, groups):
                for g in groups:
                    k, count = B.job(f"g{s + 1}_{g}")
                    if g == 0 and above(64 * u):
                        pool.wait_ge(parts_out[s], 64 * u)
                    pool.wait_ge(read[k], count)
                    nc.gpsimd.tensor_tensor(parts[s][:, g, 1, :], rest[s][:, g, :],
                                            ones[:].broadcast_to((P, W)),
                                            ALU.mult).then_inc(mid_done[s], 1)
                    pool.wait_ge(mid_done[s], 3 * u + g + 1)
                    nc.gpsimd.tensor_tensor(parts[s][:, g, 2, :], rest[s][:, g, :], parts[s][:, g, 1, :],
                                            ALU.subtract).then_inc(split_done[s], 1)

            def image(t, b):
                return t[:, 2 * b:2 * b + 2, :]

            def inverse_deviations(u, aggregated, eps_added, done):
                pool.wait_ge(aggregated, NT * (u + 1))
                nc.gpsimd.tensor_tensor(var_eps[:], mv[:, :, 1], eps[:], ALU.add).then_inc(eps_added, 1)
                pool.wait_ge(eps_added, u + 1)
                nc.gpsimd.tensor_tensor(rstd[:], var_eps[:], minus_half[:], ALU.pow).then_inc(done, 1)

            def body(B):
                i = B.i
                if B.c3:
                    u = i - 2
                    for b in range(IMGS):
                        k, count = B.last(f"down_{b}")
                        pool.wait_ge(read[k], count)
                        nc.gpsimd.tensor_tensor(image(y, b), image(down, b),
                                                down_b[:].unsqueeze(1).broadcast_to((P, 2, D)),
                                                ALU.add).then_inc(y_done, 1)
                    inverse_deviations(u, mvy_done, epsy_added, rstdy_done)
                    for b in range(IMGS):
                        pool.wait_ge(yn_done, NT * u + 2 * b + 2)
                        nc.gpsimd.tensor_tensor(image(yg, b), image(yn, b),
                                                c("gam").unsqueeze(1).broadcast_to((P, 2, D)),
                                                ALU.mult).then_inc(yg_done, 1)
                    if above(32 * u):
                        pool.wait_ge(stored, 32 * u)
                    for b in range(IMGS):
                        pool.wait_ge(yg_done, IMGS * u + b + 1)
                        nc.gpsimd.tensor_tensor(image(res, b), image(yg, b), image(h2b, b),
                                                ALU.add).then_inc(res_done, 1)
                if B.c1:
                    inverse_deviations(i, mv_done[0], eps_added[0], rstd_done[0])
                if B.a:
                    if B.c1:
                        pool.wait_ge(h1_done, IMGS * (i + 1))
                    nc.gpsimd.tensor_tensor(tok[:], tok_next[:], ones[:].unsqueeze(2).broadcast_to((P, NT, D)),
                                            ALU.mult).then_inc(tok_kept, 1)
                if B.c1:
                    split(B, 1, i, (0, 1, 2))
                if B.e:
                    k, count = B.job("var")
                    pool.wait_ge(read[k], count)
                    nc.gpsimd.tensor_tensor(rstd_img[:], var_img[:], minus_half[:, 0:IMGS],
                                            ALU.pow).then_inc(rstdimg_done, 1)
                    for b in range(IMGS):
                        pool.wait_ge(xw_done, NT * (i + 2) + 2 * b + 2)
                        nc.gpsimd.tensor_tensor(image(xg, b), image(xw, b), lnw, ALU.mult).then_inc(xg_done, 1)
                    for b in range(IMGS):
                        pool.wait_ge(xg_done, IMGS * (i + 2) + b + 1)
                        nc.gpsimd.tensor_tensor(image(xl, b), image(xg, b), lnb, ALU.add).then_inc(xl_done, 1)
                    split(B, 0, i + 2, (0, 1))
                if B.c2:
                    inverse_deviations(i - 1, mv_done[1], eps_added[1], rstd_done[1])
                if B.e:
                    split(B, 0, i + 2, (2,))
                if B.c2:
                    for b in range(IMGS):
                        nc.gpsimd.tensor_tensor(image(h2b, b), image(h2, b),
                                                c("bet").unsqueeze(1).broadcast_to((P, 2, D)),
                                                ALU.add).then_inc(h2b_done, 1)
                if B.c1:
                    pool.wait_ge(h1_done, IMGS * (i + 1))
                    nc.gpsimd.tensor_tensor(h1[:], h1_next[:], ones[:].unsqueeze(2).broadcast_to((P, NT, D)),
                                            ALU.mult).then_inc(h1_kept, 1)

            pipeline(nc.gpsimd, units, body)

        @block.scalar
        def _(act):
            act.wait_ge(const_in, 16)

            def exponentials(number):
                def evacuate_values(q):
                    act.wait_ge(av_full, QUADS * number + q + 1)
                    nc.scalar.copy(attT[:, q, :], av_bank[q % 2][:, 0:S]).then_inc(av_read, 1)

                for q in range(QUADS):
                    if above(QUADS * number + q - 1):
                        act.wait_ge(av_full, QUADS * number + q - 1)
                    for j in range(4):
                        hp, T = j // 2, j % 2
                        step = 4 * q + j
                        act.wait_ge(sc_full, STEPS * number + step + 1)
                        nc.scalar.activation(
                            probs[0:ROWS[T], q % 2, T, 2 * hp:2 * hp + 2, :],
                            sc_bank[step % 2][0:ROWS[T], 0:2 * S].rearrange("p (h s) -> p h s", h=2),
                            ACT.Exp, scale=float(DH) ** -0.5).then_inc(exp_done, 1)
                        if j == 0 and q >= 2:
                            evacuate_values(q - 2)
                evacuate_values(QUADS - 2)
                evacuate_values(QUADS - 1)

            def high_parts(B, s, u, groups):
                if 0 in groups and above(64 * u):
                    act.wait_ge(parts_out[s], 64 * u)
                for g in groups:
                    k, n = B.job(f"g{s + 1}_{g}")
                    act.wait_ge(full[k], n)
                    nc.scalar.activation(parts[s][:, g, 0, :], work[k][:, 0:W], ACT.Identity,
                                         bias=group_b[s][:, g:g + 1]).then_inc(high_done[s], 1)

            def high_max(B, s, u):
                if above(16 * u):
                    act.wait_ge(mparts_out[s], 16 * u)
                k, n = B.job(f"mt{s + 1}")
                act.wait_ge(full[k], n)
                nc.scalar.mul(mparts[s][:, 0, :], work[k][0:HEADS, 0:W], -1.0)
                nc.scalar.mul(mneg[s][:], work[k][0:HEADS, 0:W], -1.0).then_inc(read[k], 1)

            def values(B, s):
                for b in range(IMGS):
                    k, n = B.job(f"v{s + 1}_{b}")
                    act.wait_ge(full[k], n)
                    for T in range(2):
                        R = ROWS[T]
                        last = nc.scalar.copy(
                            val[s][0:R, 2 * b + T, :, 0:DH],
                            work[k][0:R, T * D:(T + 1) * D].rearrange("p (h d) -> p h d", h=HEADS))
                    last.then_inc(read[k], 1)

            def evacuate(B, name, dst):
                for half, rows in enumerate((P, DB)):
                    k, n = B.job(f"{name}_{half}")
                    act.wait_ge(full[k], n)
                    nc.scalar.copy(dst[half][0:rows, :, :].rearrange("p b s -> p (b s)"),
                                   work[k][0:rows, 0:W]).then_inc(read[k], 1)

            def body(B):
                i = B.i
                if B.c1:
                    exponentials(B.cores)
                if B.c2:
                    high_max(B, 1, i - 1)
                if B.c1:
                    evacuate(B, "xt2", xT[1])
                    high_parts(B, 1, i, (0, 1, 2))
                if B.c2:
                    exponentials(B.cores + int(B.c1))
                if B.a:
                    high_max(B, 0, i + 1)
                    values(B, 0)
                if B.e:
                    evacuate(B, "xt1", xT[0])
                if B.c2:
                    evacuate(B, "at", aT)
                if B.e:
                    high_parts(B, 0, i + 2, (0, 1))
                    high_parts(B, 0, i + 2, (2,))
                if B.c1:
                    values(B, 1)
                if B.c2:
                    evacuate(B, "ft", fT)
                if B.c2:
                    k, n = B.job("up")
                    act.wait_ge(full[k], n)
                    nc.scalar.activation(hid[:].rearrange("p b s -> p (b s)"), work[k][:, 0:W],
                                         ACT.Relu).then_inc(read[k], 1)
                    u = i - 1
                    if above(IMGS * u):
                        act.wait_ge(y_done, IMGS * u)
                    for b in range(IMGS):
                        k, n = B.job(f"down_{b}")
                        act.wait_ge(full[k], n)
                        nc.scalar.copy(down[0:ROWS[0], 2 * b, :], work[k][0:ROWS[0], 0:D])
                        nc.scalar.copy(down[0:ROWS[1], 2 * b + 1, :],
                                       work[k][0:ROWS[1], D:2 * D]).then_inc(read[k], 1)

            pipeline(nc.scalar, units, body)

        @block.vector
        def _(dve):
            for s in range(2):
                nc.vector.memset(stack_k[s][KS:KM, :, :], 1.0)
                nc.vector.memset(val[s][:, :, :, DH:2 * DH], 1.0)
            for t in (xT[0][1], xT[1][1], aT[1], fT[1]):
                nc.vector.memset(t[DB:P, :, :], 0.0)
            for t in (mv_img, mv, tok_next, xw, att, h2, down, yn):
                nc.vector.memset(t[:], 0.0)
            nc.vector.memset(eps[:], LN_EPS)
            nc.vector.memset(ones[:], 1.0)
            nc.vector.memset(minus_half[:], -0.5).then_inc(zeroed, 1)
            dve.wait_ge(zeroed, 1)
            for t in (xT[0][1], xT[1][1], aT[1], fT[1]):
                last = nc.vector.memset(t[DB:DB + 1, :, :], 1.0)
            last.then_inc(zeroed, 1)
            dve.wait_ge(const_in, 16)
            dve.wait_ge(fold_full, 2)
            nc.vector.tensor_copy(down_w[:], work[0][:, 0:D])
            nc.vector.tensor_copy(down_b[:], work[1][:, 0:D]).then_inc(fold_read, 1)
            dve.wait_ge(set_up, 1)

            def maxima(passes, step):
                q, j = divmod(step, 4)
                b, quad = divmod(q, QUADS // IMGS)
                hp, T = j // 2, j % 2
                h = 4 * quad + 2 * hp
                dve.wait_ge(mx_full, STEPS * passes + step + 1)
                nc.vector.tensor_reduce(
                    maxes[0:ROWS[T], 2 * b + T, h:h + 2],
                    mx_bank[step % 2][0:ROWS[T], 0:2 * S].rearrange("p (h s) -> p h s", h=2),
                    AX.X, ALU.max).then_inc(mx_read, 1)

            def normalise(B, s, u, b):
                for T, R in enumerate(ROWS):
                    n = 2 * b + T
                    k, count = B.job(f"ot{s + 1}_{n}")
                    dve.wait_ge(full[k], count)
                    nc.vector.reciprocal(
                        rden[0:R, n, :],
                        work[k][0:R, 0:2 * D].rearrange("p (h d) -> p h d", h=HEADS)[:, :, DH]
                    ).then_inc(rden_done[s], 1)
                for T, R in enumerate(ROWS):
                    n = 2 * b + T
                    k, count = B.job(f"ot{s + 1}_{n}")
                    dve.wait_ge(rden_done[s], NT * u + n + 1)
                    nc.vector.tensor_tensor(
                        att[0:R, n, :].rearrange("p (h d) -> p h d", h=HEADS),
                        work[k][0:R, 0:2 * D].rearrange("p (h d) -> p h d", h=HEADS)[:, :, 0:DH],
                        rden[0:R, n, :].unsqueeze(2).broadcast_to((R, HEADS, DH)),
                        ALU.mult).then_inc(read[k], 1)

            def max_rest(B, s, u):
                k, n = B.job(f"mt{s + 1}")
                dve.wait_ge(read[k], n)
                nc.vector.tensor_tensor(mrest[s][:], mneg[s][:], mparts[s][:, 0, :],
                                        ALU.subtract).then_inc(mrest_done[s], 1)

            def max_split(B, s, u):
                dve.wait_ge(mrest_done[s], u + 1)
                nc.vector.tensor_copy(mparts[s][:, 1, :], mrest[s][:]).then_inc(mmid_done[s], 1)
                dve.wait_ge(mmid_done[s], u + 1)
                nc.vector.tensor_tensor(mparts[s][:, 2, :], mrest[s][:], mparts[s][:, 1, :],
                                        ALU.subtract).then_inc(msplit_done[s], 1)

            def rests(B, s, u, groups):
                if 0 in groups and above(3 * u):
                    dve.wait_ge(split_done[s], 3 * u)
                for g in groups:
                    k, n = B.job(f"g{s + 1}_{g}")
                    dve.wait_ge(high_done[s], 3 * u + g + 1)
                    nc.vector.scalar_tensor_tensor(rest[s][:, g, :], work[k][:, 0:W],
                                                   group_b[s][:, g:g + 1], parts[s][:, g, 0, :],
                                                   ALU.add, ALU.subtract).then_inc(read[k], 1)

            def aggregate(stats_done, u, aggregate_tile, aggregated):
                dve.wait_ge(stats_done, NT * (u + 1))
                nc.vector.memset(spare[:], 0.0)
                for n, b, T, R in tiles():
                    aggregate_tile(n, b, T, R).then_inc(aggregated, 1)

            def row_statistics(src, u, stats_done, tiles_):
                for n, b, T, R in tiles_:
                    nc.vector.bn_stats(bst[0:R, n, :], src[0:R, n, :]).then_inc(stats_done, 1)

            def row_aggregates(u, stats_done, aggregated):
                aggregate(stats_done, u,
                          lambda n, b, T, R: nc.vector.bn_aggr(mv[0:R, n, :], bst[0:R, n, :]), aggregated)

            def row_norm(src, dst, done, tiles_):
                for n, b, T, R in tiles_:
                    nc.vector.tensor_scalar(dst[0:R, n, :], src[0:R, n, :], mv[0:R, n, 0:1],
                                            rstd[0:R, n:n + 1], ALU.subtract, ALU.mult).then_inc(done, 1)

            def output_rows(B, step):
                u = B.i - 2
                if step in (4, 6):
                    dve.wait_ge(y_done, IMGS * u + (step - 4) // 2 + 1)
                    row_statistics(y, u, bsty_done, tiles()[step - 4:step - 2])
                if step == 7:
                    row_aggregates(u, bsty_done, mvy_done)
                if step == 11:
                    if above(IMGS * u):
                        dve.wait_ge(yg_done, IMGS * u)
                    dve.wait_ge(rstdy_done, u + 1)
                if step in (11, 13):
                    row_norm(y, yn, yn_done, tiles()[step - 11:step - 9])

            def embedded_images(B, step):
                i = B.i
                if step == 2:
                    k, count = B.job("mean")
                    dve.wait_ge(full[k], count)
                    nc.vector.tensor_copy(mean_img[:], work[k][:, 0:IMGS])
                    nc.vector.tensor_tensor(dev_img[:], mv_img[:, :, :, 0],
                                            work[k][:, 0:IMGS].unsqueeze(1).broadcast_to((P, 2, IMGS)),
                                            ALU.subtract).then_inc(read[k], 1)
                if step == 4:
                    k, count = B.job("mean")
                    dve.wait_ge(read[k], count)
                    nc.vector.tensor_tensor(sq_img[:], dev_img[:], dev_img[:], ALU.mult).then_inc(sq_done, 1)
                if step == 6:
                    dve.wait_ge(sq_done, i + 3)
                    nc.vector.tensor_tensor(e_img[:], sq_img[:], mv_img[:, :, :, 1],
                                            ALU.add).then_inc(e_done, 1)
                if step == 12:
                    k, count = B.job("var")
                    dve.wait_ge(full[k], count)
                    nc.vector.tensor_scalar(var_img[:], work[k][:, 0:IMGS], LN_EPS, None,
                                            ALU.add).then_inc(read[k], 1)
                if step == 13:
                    if above(IMGS * (i + 2)):
                        dve.wait_ge(xg_done, IMGS * (i + 2))
                    dve.wait_ge(rstdimg_done, i + 3)
                if step in (13, 15, 17, 19):
                    n, b, T, R = tiles()[(step - 13) // 2]
                    nc.vector.tensor_scalar(xw[0:R, n, :], tok_next[0:R, n, :], mean_img[0:R, b:b + 1],
                                            rstd_img[0:R, b:b + 1], ALU.subtract,
                                            ALU.mult).then_inc(xw_done, 1)

            def add_rows(B, name, b, dst, other):
                k, count = B.job(f"{name}_{b}")
                dve.wait_ge(full[k], count)
                for T in range(2):
                    R = ROWS[T]
                    last = nc.vector.tensor_tensor(dst[0:R, 2 * b + T, :], work[k][0:R, T * D:(T + 1) * D],
                                                   other(2 * b + T, T, R), ALU.add)
                last.then_inc(read[k], 1)

            def embedding(B, b):
                add_rows(B, "emb", b, tok_next, lambda n, T, R: pos_bias[0:R, T, :])
                k, count = B.job(f"emb_{b}")
                dve.wait_ge(read[k], count)
                for T in range(2):
                    n, R = 2 * b + T, ROWS[T]
                    nc.vector.bn_stats(bst1[0:R, n, :], tok_next[0:R, n, :]).then_inc(bst1_done, 1)

            def body(B):
                i = B.i
                for step in range(STEPS):
                    if B.c2 and step >= AHEAD:
                        maxima(B.passes, step)
                    if B.c3:
                        output_rows(B, step)
                if B.c1:
                    if above(i):
                        dve.wait_ge(h1_kept, i)
                    dve.wait_ge(tok_kept, i + 1)
                    for b in range(IMGS):
                        normalise(B, 0, i, b)
                        for n in (2 * b, 2 * b + 1):
                            k, count = B.job(f"ot1_{n}")
                            dve.wait_ge(read[k], count)
                        nc.vector.tensor_tensor(h1_next[:, 2 * b:2 * b + 2, :], att[:, 2 * b:2 * b + 2, :],
                                                tok[:, 2 * b:2 * b + 2, :], ALU.add).then_inc(h1_done, 1)
                        dve.wait_ge(h1_done, IMGS * i + b + 1)
                        row_statistics(h1_next, i, bst_done[0], tiles()[2 * b:2 * b + 2])
                    row_aggregates(i, bst_done[0], mv_done[0])
                if B.c2:
                    max_rest(B, 1, i - 1)
                    max_split(B, 1, i - 1)
                if B.c1:
                    dve.wait_ge(rstd_done[0], i + 1)
                    row_norm(h1_next, xn1, xn_done[0], tiles())
                if B.e:
                    if B.a:
                        dve.wait_ge(tok_kept, i + 2)
                    embedding(B, 0)
                    embedding(B, 1)
                    aggregate(bst1_done, i + 2,
                              lambda n, b, T, R: nc.vector.bn_aggr(mv_img[0:R, T, b, :], bst1[0:R, n, :]),
                              mvimg_done)
                if B.a:
                    maxima(B.passes + int(B.c2), 0)
                    maxima(B.passes + int(B.c2), 1)
                if B.c1:
                    rests(B, 1, i, (0, 1))
                for step in range(STEPS):
                    if B.a and step >= AHEAD:
                        maxima(B.passes + int(B.c2), step)
                    if B.c1 and step == AHEAD:
                        rests(B, 1, i, (2,))
                    if B.e:
                        embedded_images(B, step)
                if B.c2:
                    normalise(B, 1, i - 1, 0)
                    normalise(B, 1, i - 1, 1)
                if B.a:
                    max_rest(B, 0, i + 1)
                    max_split(B, 0, i + 1)
                if B.e:
                    rests(B, 0, i + 2, (0, 1))
                if B.c2:
                    u = i - 1
                    if above(IMGS * u):
                        dve.wait_ge(h2b_done, IMGS * u)
                    dve.wait_ge(h1_kept, i)
                    for b in range(IMGS):
                        add_rows(B, "proj", b, h2, lambda n, T, R: h1[0:R, n, :])
                        k, count = B.job(f"proj_{b}")
                        dve.wait_ge(read[k], count)
                        row_statistics(h2, u, bst_done[1], tiles()[2 * b:2 * b + 2])
                    row_aggregates(u, bst_done[1], mv_done[1])
                if B.e:
                    rests(B, 0, i + 2, (2,))
                if B.c2:
                    dve.wait_ge(rstd_done[1], u + 1)
                    row_norm(h2, xn2, xn_done[1], tiles())
                if B.c1:
                    maxima(B.passes + int(B.c2) + int(B.a), 0)
                    maxima(B.passes + int(B.c2) + int(B.a), 1)

            pipeline(nc.vector, units, body)

        @block.tensor
        def _(pe):
            pe.wait_ge(const_in, 16)
            pe.wait_ge(zeroed, 2)

            for k, (name, n) in enumerate((("w2", INNER), ("b2", P))):
                for half in range(2):
                    last = nc.tensor.matmul(work[k][:, 0:D], c(name, 2)[:, half, :], c("wo", 2)[:, half, :],
                                            start=half == 0, stop=half == 1)
                last.then_inc(fold_full, 1)
            pe.wait_ge(fold_read, 1)

            def begin(B, name):
                k, n = B.job(name)
                if above(n - 1):
                    pe.wait_ge(read[k], n - 1)
                return k, work[k]

            def was_read(B, name):
                k, n = B.job(name)
                pe.wait_ge(read[k], n)

            def step_of(step):
                q, j = divmod(step, 4)
                b, quad = divmod(q, QUADS // IMGS)
                return b, 4 * quad + 2 * (j // 2), j % 2

            def part(stack, rows, h, b, cols):
                return stack[0:rows, h, b * S + cols.start:b * S + cols.stop]

            def for_maxima(maxima, step):
                s, u, number = maxima
                b, h0, T = step_of(step)
                if step == 0:
                    pe.wait_ge(stack_in[s], 192 * (u + 1))
                if above(STEPS * number + step - 1):
                    pe.wait_ge(mx_read, STEPS * number + step - 1)
                for h in (0, 1):
                    last = nc.tensor.matmul(
                        mx_bank[step % 2][0:ROWS[T], h * S:(h + 1) * S],
                        part(stack_q[s], KS, h0 + h, b, COLS[T]),
                        part(stack_k[s], KS, h0 + h, b, slice(0, S)), start=True, stop=True)
                last.then_inc(mx_full, 1)

            def core(scores, maxima, between):
                for q in range(QUADS):
                    for j in range(4):
                        step = 4 * q + j
                        b, h0, T = step_of(step)
                        if maxima is not None and step + AHEAD < STEPS:
                            for_maxima(maxima, step + AHEAD)
                        if scores is not None:
                            s, u, number, lent = scores
                            if step == 0:
                                pe.wait_ge(mrows_in[s], 16 * (u + 1))
                            if above(STEPS * number + step - 1):
                                pe.wait_ge(exp_done, STEPS * number + step - 1)
                            for h in (0, 1):
                                last = nc.tensor.matmul(
                                    sc_bank[step % 2][0:ROWS[T], h * S:(h + 1) * S],
                                    part(stack_k[s], KM, h0 + h, b, COLS[T]),
                                    part(stack_q[s], KM, h0 + h, b, slice(0, S)), start=True, stop=True)
                            last.then_inc(sc_full, 1)
                        if scores is not None and q > 0 and j % 2 == 1:
                            times_values(scores, q - 1, j // 2)
                        between(step)

            def times_values(scores, q, T):
                s, u, number, lent = scores
                b, quad = divmod(q, QUADS // IMGS)
                R = ROWS[T]
                if T == 0:
                    pe.wait_ge(exp_done, STEPS * number + 4 * (q + 1))
                    if above(QUADS * number + q - 1):
                        pe.wait_ge(av_read, QUADS * number + q - 1)
                    if q == 1 and above(lent):
                        pe.wait_ge(read[LENT], lent)
                for h in range(4):
                    last = nc.tensor.matmul(av_bank[q % 2][2 * DH * h:2 * DH * (h + 1), 0:S],
                                            val[s][0:R, 2 * b + T, 4 * quad + h, :],
                                            probs[0:R, q % 2, T, h, :], start=T == 0, stop=T == 1)
                if T == 1:
                    last.then_inc(av_full, 1)

            def attention_rows(B, s, n):
                b, T = divmod(n, 2)
                k, ps = begin(B, f"ot{s + 1}_{n}")
                for quad in range(3):
                    last = nc.tensor.transpose(ps[0:ROWS[T], quad * P:(quad + 1) * P],
                                               attT[:, 3 * b + quad, COLS[T]], ident)
                last.then_inc(full[k], 1)

            def max_columns(B, s, passes):
                k, ps = begin(B, f"mt{s + 1}")
                pe.wait_ge(mx_read, STEPS * (passes + 1))
                for n, b, T, R in tiles():
                    last = nc.tensor.transpose(ps[0:HEADS, b * S + COLS[T].start:b * S + COLS[T].stop],
                                               maxes[0:R, n, :], ident[0:R, 0:R])
                last.then_inc(full[k], 1)

            def transposed(B, name, src, src_done):
                banks = [begin(B, f"{name}_{half}") for half in range(2)]
                for half, (k, ps) in enumerate(banks):
                    for n, b, T, R in tiles():
                        if half == 0:
                            src_done(n)
                        width = (P, DB)[half]
                        last = nc.tensor.transpose(ps[0:width, b * S + COLS[T].start:b * S + COLS[T].stop],
                                                   src[0:R, n, half * P:half * P + width],
                                                   ident[0:R, 0:R])
                    last.then_inc(full[k], 1)

            def groups(B, s, groups_):
                for g in groups_:
                    k, ps = begin(B, f"g{s + 1}_{g}")
                    halves = ([1] if g == 2 else [0]) if s == 0 else [0, 1]
                    for half in halves:
                        last = nc.tensor.matmul(ps[:, 0:W], group_w[s][:, half, g * P:(g + 1) * P],
                                                xT[s][half][:].rearrange("p b s -> p (b s)"),
                                                start=half == halves[0], stop=half == halves[-1])
                    last.then_inc(full[k], 1)

            def rows_times(B, name, xT_, w):
                for b in range(IMGS):
                    k, ps = begin(B, f"{name}_{b}")
                    for T in range(2):
                        for half in range(len(xT_)):
                            last = nc.tensor.matmul(ps[0:ROWS[T], T * D:(T + 1) * D],
                                                    xT_[half][:, b, COLS[T]], w[half],
                                                    start=half == 0, stop=half == len(xT_) - 1)
                    last.then_inc(full[k], 1)

            def image_sum(B, name, rhs):
                k, ps = begin(B, name)
                for T in range(2):
                    last = nc.tensor.matmul(ps[:, 0:IMGS], avg[0:ROWS[T], :], rhs(T),
                                            start=T == 0, stop=T == 1)
                last.then_inc(full[k], 1)

            def embed(B, b):
                k, ps = begin(B, f"emb_{b}")
                for T in range(2):
                    for ch in range(CH):
                        last = nc.tensor.matmul(ps[0:ROWS[T], T * D:(T + 1) * D],
                                                xin[:, b, ch, COLS[T]], wm[:, ch, :],
                                                start=ch == 0, stop=ch == CH - 1)
                last.then_inc(full[k], 1)

            def whole_core(B, s, scores, maxima, between):
                core(scores, maxima, between)
                if scores is not None:
                    quads = QUADS * scores[2]
                    pe.wait_ge(av_read, quads + QUADS // IMGS)
                    attention_rows(B, s, 0)
                    times_values(scores, QUADS - 1, 0)
                    times_values(scores, QUADS - 1, 1)
                    attention_rows(B, s, 1)
                    pe.wait_ge(av_read, quads + QUADS)
                if maxima is not None:
                    max_columns(B, 1 - s, maxima[2])
                if scores is not None:
                    attention_rows(B, s, 2)
                    attention_rows(B, s, 3)

            def body(B):
                i = B.i
                maxima_2 = (0, i + 1, B.passes + int(B.c2)) if B.a else None
                whole_core(B, 0, (0, i, B.cores, B.lent(0)) if B.c1 else None, (1, i - 1, B.passes) if B.c2 else None,
                           lambda step: None)
                if B.e:
                    pe.wait_ge(x_in, 16 * (i + 3))
                    embed(B, 0)
                if B.c1:
                    transposed(B, "xt2", xn1, lambda n: pe.wait_ge(xn_done[0], NT * i + n + 1))
                if B.e:
                    embed(B, 1)
                if B.a:
                    for_maxima(maxima_2, 0)
                    for_maxima(maxima_2, 1)
                if B.c1:
                    was_read(B, "xt2_0")
                    was_read(B, "xt2_1")
                    groups(B, 1, (0, 1, 2))

                def image_sums(step):
                    if B.e and step == 1:
                        pe.wait_ge(mvimg_done, NT * (i + 3))
                        image_sum(B, "mean", lambda T: mv_img[0:ROWS[T], T, :, 0])
                    if B.e and step == 10:
                        pe.wait_ge(e_done, i + 3)
                        image_sum(B, "var", lambda T: e_img[0:ROWS[T], T, :])

                whole_core(B, 1, (1, i - 1, B.cores + int(B.c1), B.lent(1)) if B.c2 else None,
                           maxima_2, image_sums)
                if B.a:
                    rows_times(B, "v1", xT[0], [value_w[0][:, 0, :], value_w[0][:, 1, :]])
                if B.e:
                    transposed(B, "xt1", xl, lambda n: pe.wait_ge(xl_done, IMGS * (i + 2) + n // 2 + 1))
                if B.c2:
                    transposed(B, "at", att, lambda n: was_read(B, f"ot2_{n}"))
                if B.e:
                    was_read(B, "xt1_0")
                    was_read(B, "xt1_1")
                    groups(B, 0, (0, 1))
                if B.c2:
                    was_read(B, "at_0")
                    was_read(B, "at_1")
                    rows_times(B, "proj", aT, [proj_w[:, 0, :], proj_w[:, 1, :]])
                if B.e:
                    groups(B, 0, (2,))
                if B.c1:
                    rows_times(B, "v2", xT[1], [value_w[1][:, 0, :], value_w[1][:, 1, :]])
                if B.c2:
                    u = i - 1
                    transposed(B, "ft", xn2, lambda n: pe.wait_ge(xn_done[1], NT * u + n + 1))
                if B.c1:
                    for_maxima((1, i, B.passes + int(B.c2) + int(B.a)), 0)
                if B.c2:
                    was_read(B, "ft_0")
                    was_read(B, "ft_1")
                    k, ps = begin(B, "up")
                    for half in range(2):
                        last = nc.tensor.matmul(ps[:, 0:W], up_w[:, half, :],
                                                fT[half][:].rearrange("p b s -> p (b s)"),
                                                start=half == 0, stop=half == 1)
                    last.then_inc(full[k], 1)
                if B.c1:
                    for_maxima((1, i, B.passes + int(B.c2) + int(B.a)), 1)
                if B.c2:
                    was_read(B, "up")
                    rows_times(B, "down", [hid], [down_w[:]])

            pipeline(nc.tensor, units, body)


def kernel(x, L0_tok_W_map, L0_tok_b_map, L0_tok_class_token, L0_tok_ln_w, L0_tok_ln_b, L0_tok_Wq,
           L0_tok_bq, L0_tok_Wk, L0_tok_bk, L0_tok_Wv, L0_tok_bv, L0_attn_w_attn, L0_attn_b_attn,
           L0_attn_w_proj, L0_attn_b_proj, L0_ffn_W1, L0_ffn_b1, L0_ffn_W2, L0_ffn_b2, L0_ffn_Wo,
           L0_ffn_bo, L0_ffn_gamma, L0_ffn_beta):
    import numpy as np
    import concourse.bacc as bacc
    from concourse.bass_utils import run_bass_kernel_spmd

    f32 = np.float32
    images = np.asarray(x)
    units = images.shape[0] // IMGS

    patches = images.reshape(units, IMGS, S - 1, CH, P)
    x_host = np.zeros((units, P, IMGS, CH, S), f32)
    x_host[..., 1:] = patches.transpose(0, 4, 1, 3, 2)

    packed = np.zeros((P, NCONST), f32)

    def put(name, value):
        at, n = CONST[name]
        value = np.asarray(value)
        chunks = value[None] if value.ndim == 2 else value
        per = n // len(chunks)
        for k, v in enumerate(chunks):
            packed[:v.shape[0], at + k * per:at + k * per + v.shape[1]] = v

    def row_tiles(a):
        t = np.zeros((2, P, D), f32)
        t[0], t[1, :S - P] = a[:P], a[P:]
        return t

    def contraction(a, bias=None):
        t = np.zeros((2, P, a.shape[1]), f32)
        t[0], t[1, :DB] = a[:P], a[P:]
        if bias is not None:
            t[1, DB] = bias
        return t

    def blocks(w):
        t = np.zeros((D, D), f32)
        for h in range(HEADS):
            t[h * DH:(h + 1) * DH, h * DH:(h + 1) * DH] = w[h].T
        return t

    def grouped(q, k):
        def heads(a, h0, h1):
            a = a.reshape(a.shape[:-1] + (HEADS, DH))[..., h0:h1, :]
            return np.swapaxes(a, -1, -2).reshape(a.shape[:-2] + (-1,))
        return np.concatenate([heads(q, 0, HG), heads(k, 0, HG), heads(q, HG, HEADS),
                               heads(k, HG, HEADS)], axis=-1)

    i = np.arange(S, dtype=f32)[:, None]
    j = np.arange(D, dtype=f32)[None, :]
    pos = np.where((np.arange(D) % 2 == 0)[None, :], np.sin(i / np.power(f32(10000.0), j / f32(D))),
                   np.cos(i / np.power(f32(10000.0), (j - f32(1.0)) / f32(D)))).astype(f32)
    tokb = np.zeros((S, D), f32)
    tokb[0], tokb[1:] = np.asarray(L0_tok_class_token)[0], np.asarray(L0_tok_b_map)

    wq, wk, wv = (blocks(np.asarray(w)) for w in (L0_tok_Wq, L0_tok_Wk, L0_tok_Wv))
    w_attn, b_attn = np.asarray(L0_attn_w_attn), np.asarray(L0_attn_b_attn)

    put("wm", np.asarray(L0_tok_W_map).T.reshape(CH, P, D))
    put("pos", row_tiles(pos))
    put("tokb", row_tiles(tokb))
    put("lnw", row_tiles(np.asarray(L0_tok_ln_w)))
    put("lnb", row_tiles(np.asarray(L0_tok_ln_b)))
    put("g1", contraction(grouped(wq, wk)))
    put("g2", contraction(grouped(w_attn[:, :D], w_attn[:, D:2 * D])))
    put("gb1", grouped(np.asarray(L0_tok_bq).reshape(D), np.asarray(L0_tok_bk).reshape(D)).reshape(3, P).T)
    put("gb2", grouped(b_attn[:D], b_attn[D:2 * D]).reshape(3, P).T)
    put("wv1", contraction(wv, np.asarray(L0_tok_bv).reshape(D)))
    put("wv2", contraction(w_attn[:, 2 * D:], b_attn[2 * D:]))
    put("wp", contraction(np.asarray(L0_attn_w_proj), np.asarray(L0_attn_b_proj)))
    put("w1", contraction(np.asarray(L0_ffn_W1).T, np.asarray(L0_ffn_b1)))
    put("w2", contraction(np.asarray(L0_ffn_W2)))
    put("wo", contraction(np.asarray(L0_ffn_Wo).T, np.asarray(L0_ffn_bo)))
    put("b2", contraction(np.broadcast_to(np.asarray(L0_ffn_b2)[:, None], (D, P)), np.ones(P, f32)))
    put("gam", np.broadcast_to(np.asarray(L0_ffn_gamma), (P, D)))
    put("bet", np.broadcast_to(np.asarray(L0_ffn_beta), (P, D)))
    put("ident", np.eye(P, dtype=f32))
    put("avg", np.full((P, P), 1.0 / S, f32))

    nc = bacc.Bacc("TRN2", target_bir_lowering=False, num_devices=1)
    x_dram = nc.dram_tensor("x_dram", x_host.shape, F32, kind="ExternalInput").ap()
    const_dram = nc.dram_tensor("const_dram", packed.shape, F32, kind="ExternalInput").ap()
    out_dram = nc.dram_tensor("out_dram", (units, IMGS, S, D), F32, kind="ExternalOutput").ap()
    vit_tower(nc, x_dram, const_dram, out_dram)
    result = run_bass_kernel_spmd(nc, [{"x_dram": x_host, "const_dram": packed}], core_ids=[0])
    return result.results[0]["out_dram"].reshape(images.shape[0], S, D)
```

```python
from contextlib import ExitStack

import concourse.bass as bass
from concourse import mybir

F32 = mybir.dt.float32
BF16 = mybir.dt.bfloat16
ALU = mybir.AluOpType
ACT = mybir.ActivationFunctionType
AX = mybir.AxisListType

P = 128
IMGS = 2
S = 197
D = 192
HEADS = 12
DH = D // HEADS
DB = D - P
PIX = 768
CH = PIX // P
INNER = 128
LN_EPS = 1e-5
ROWS = [P, S - P]
COLS = [slice(0, P), slice(P, S)]
NT = 2 * IMGS
W = IMGS * S
PARTS = 3
SLOT_Q = [0, 0, 0, 1, 1, 2]
SLOT_K = [0, 1, 2, 0, 1, 0]
KS = len(SLOT_Q) * DH
KM = P - PARTS
QUADS = IMGS * HEADS // 4
STEPS = 4 * QUADS
HG = 8

_SIZES = [("wm", CH * D), ("pos", 2 * D), ("tokb", 2 * D), ("lnw", 2 * D), ("lnb", 2 * D),
          ("g1", 2 * 3 * P), ("g2", 2 * 3 * P), ("gb1", 3), ("gb2", 3), ("wv1", 2 * D),
          ("wv2", 2 * D), ("wp", 2 * D), ("w1", 2 * INNER), ("w2", 2 * INNER), ("wo", 2 * D),
          ("b2", 2 * P), ("bv1", D), ("gam", D), ("bet", D), ("ident", P), ("avg", P)]
CONST = {}
_at = 0
for _name, _n in _SIZES:
    CONST[_name] = (_at, _n)
    _at += _n
NCONST = _at

JOBS = ([("down_0", "c3"), ("down_1", "c3"), ("", None)]
        + [("ot1_0", "c1"), ("ot1_1", "c1"), ("mt2", "c2"), ("ot1_2", "c1"), ("ot1_3", "c1")]
        + [("emb_0", "e"), ("emb_1", "e"), ("xt2_0", "c1"), ("xt2_1", "c1")]
        + [(f"g2_{g}", "c1") for g in range(3)] + [("mean", "e"), ("var", "e"), ("", None)]
        + [("ot2_0", "c2"), ("ot2_1", "c2"), ("mt1", "a"), ("ot2_2", "c2"), ("ot2_3", "c2")]
        + [("v1_0", "a"), ("v1_1", "a"), ("xt1_0", "e"), ("xt1_1", "e"), ("at_0", "c2"), ("at_1", "c2")]
        + [("g1_0", "e"), ("proj_0", "c2"), ("proj_1", "c2"), ("g1_1", "e"), ("g1_2", "e")]
        + [("v2_0", "c1"), ("v2_1", "c1"), ("ft_0", "c2"), ("ft_1", "c2")]
        + [("up", "c2")])
AHEAD = QUADS
EMBED_MAXIMA = [(0, 5), (1, 1), (1, 4), (1, 5)]
SPILLS = 16 * 4 * PARTS
LOADS = 16 * 2 * 3
assert STEPS == AHEAD + 3 * QUADS
NBANK = 3
LENT = NBANK - 1
FIRST = 3


class Body:

    def __init__(self, i, units, before, passes, cores, full=False):
        self.i, self.before, self.passes, self.cores = i, before, passes, cores
        self.c1, self.c2, self.c3, self.a, self.e = (full or 0 <= i + k < units
                                                     for k in (0, -1, -2, 1, 2))

    def has(self, unit):
        return {"c1": self.c1, "c2": self.c2, "c3": self.c3, "a": self.a, "e": self.e, None: False}[unit]

    def jobs_per_bank(self):
        n = [0] * NBANK
        for k, (_, unit) in enumerate(JOBS):
            n[k % NBANK] += self.has(unit)
        return n

    def job(self, name):
        done = list(self.before)
        for k, (other, unit) in enumerate(JOBS):
            done[k % NBANK] = done[k % NBANK] + int(self.has(unit))
            if other == name:
                return k % NBANK, done[k % NBANK]
        raise KeyError(name)

    def last(self, name):
        k = [other for other, _ in JOBS].index(name) % NBANK
        return k, self.before[k]

    def lent(self, s):
        stop = JOBS.index((f"ot{s + 1}_0", ("c1", "c2")[s]))
        return self.before[LENT] + sum(self.has(unit) for _, unit in JOBS[LENT:stop:NBANK])

    def after(self, times=1):
        return ([x + times * n for x, n in zip(self.before, self.jobs_per_bank())],
                self.passes + times * (self.c2 + self.a), self.cores + times * (self.c1 + self.c2))


def pipeline(eng, units, emit):
    before = ([0] * NBANK, 0, 0)
    for i in range(-2, FIRST):
        body = Body(i, units, *before)
        emit(body)
        before = body.after()
    loops = units - 2 - FIRST
    full = Body(FIRST, units, *before, full=True)
    with eng.Fori(FIRST, FIRST + loops) as i:
        t = i - FIRST
        emit(Body(i, units, [x + t * m for x, m in zip(before[0], full.jobs_per_bank())],
                  before[1] + t * 2, before[2] + t * 2, full=True))
    before = full.after(loops)
    for i in range(units - 2, units + 2):
        body = Body(i, units, *before)
        emit(body)
        before = body.after()


def above(value):
    return not isinstance(value, int) or value > 0


def vit_tower(nc: bass.Bass, x, consts, out):
    units = x.shape[0]
    scratch = [[nc.dram_tensor(f"parts_{o}{s}", (PARTS, DH * HEADS, W), BF16).ap() for o in "qk"]
               for s in (1, 2)]
    scratch_max = [nc.dram_tensor(f"parts_max{s}", (PARTS, HEADS, W), BF16).ap() for s in (1, 2)]

    with ExitStack() as ctx:
        def sb(name, shape, dt=F32):
            return ctx.enter_context(nc.sbuf_tensor(name, shape, dt))

        def bank(name):
            return ctx.enter_context(nc.psum_tensor(name, [P, 512], F32))

        def sem(name):
            return ctx.enter_context(nc.semaphore(name))

        def sem2(name):
            return [sem(f"{name}{s}") for s in (1, 2)]

        const = sb("const", [P, NCONST])

        def c(name, *split):
            at, n = CONST[name]
            v = const[:, at:at + n]
            return v.rearrange("p (a n) -> p a n", a=split[0]) if split else v

        wm, lnw, lnb = c("wm", CH), c("lnw", 2), c("lnb", 2)
        group_w, group_b = [c("g1", 2), c("g2", 2)], [c("gb1"), c("gb2")]
        value_w, proj_w, up_w = [c("wv1", 2), c("wv2", 2)], c("wp", 2), c("w1", 2)
        ident, avg = c("ident"), c("avg")
        pos_bias = sb("pos_bias", [P, 2, D])
        down_w = sb("down_w", [P, D])
        down_b = sb("down_b", [P, D])

        xin = sb("xin", [P, IMGS, CH, S])
        tok_next = sb("tok_next", [P, NT, D])
        tok = sb("tok", [P, NT, D])
        bst = sb("bst", [P, NT, 6])
        bst1 = sb("bst1", [P, NT, 6])
        mv_img = sb("mv_img", [P, 2, IMGS, 2])
        dev_img = sb("dev_img", [P, 2, IMGS])
        sq_img = sb("sq_img", [P, 2, IMGS])
        e_img = sb("e_img", [P, 2, IMGS])
        mean_img = sb("mean_img", [P, IMGS])
        var_img = sb("var_img", [P, IMGS])
        rstd_img = sb("rstd_img", [P, IMGS])
        xd = xg = sb("xd_xg", [P, NT, D])
        xw = xl = sb("xw_xl", [P, NT, D])
        xT = [[sb(f"xT{s}{k}", [P, IMGS, S]) for k in "AB"] for s in (1, 2)]
        aT = [sb(f"aT{k}", [P, IMGS, S]) for k in "AB"]
        fT = [sb(f"fT{k}", [P, IMGS, S]) for k in "AB"]
        parts = [sb(f"parts{s}", [P, 3, PARTS, W], BF16) for s in (1, 2)]
        rest = [sb(f"rest{s}", [P, 3, W]) for s in (1, 2)]
        stack_q = [sb(f"stack_q{s}", [P, HEADS, W], BF16) for s in (1, 2)]
        stack_k = [sb(f"stack_k{s}", [P, HEADS, W], BF16) for s in (1, 2)]
        maxes = sb("maxes", [P, NT, HEADS])
        mparts = [sb(f"mparts{s}", [HEADS, PARTS, W], BF16) for s in (1, 2)]
        mneg = [sb(f"mneg{s}", [HEADS, W]) for s in (1, 2)]
        mrest = [sb(f"mrest{s}", [HEADS, W]) for s in (1, 2)]
        val = [sb(f"val{s}", [P, NT, HEADS, 2 * DH]) for s in (1, 2)]
        probs = sb("probs", [P, 2, 2, 4, S])
        attT = sb("attT", [P, QUADS, S])
        rden = sb("rden", [P, NT, HEADS])
        att = sb("att", [P, NT, D])
        h1_next = sb("h1_next", [P, NT, D])
        h1 = sb("h1", [P, NT, D])
        mv = sb("mv", [P, NT, 2])
        rstd = sb("rstd", [P, NT])
        var_eps = sb("var_eps", [P, NT])
        spare = sb("spare", [P, 1])
        eps = sb("eps", [P, NT])
        ones = sb("ones", [P, 1])
        minus_half = sb("minus_half", [P, NT])
        xn1 = sb("xn1", [P, NT, D])
        xn2 = sb("xn2", [P, NT, D])
        h2 = sb("h2", [P, NT, D])
        h2b = sb("h2b", [P, NT, D])
        hid = sb("hid", [P, IMGS, S])
        down = sb("down", [P, NT, D])
        y = sb("y", [P, NT, D])
        yn = sb("yn", [P, NT, D])
        yg = sb("yg", [P, NT, D])
        res = sb("res", [P, NT, D])

        mx_bank = [bank("mx_bank0"), bank("mx_bank1")]
        sc_bank = [bank("sc_bank0"), bank("sc_bank1")]
        work = [bank(f"work{k}") for k in range(NBANK)]
        av_bank = [bank("av_bank"), work[LENT]]

        const_in = sem("const_in")
        x_in = sem("x_in")
        parts_out = sem2("parts_out")
        stack_in = sem2("stack_in")
        mparts_out = sem2("mparts_out")
        mrows_in = sem2("mrows_in")
        stored = sem("stored")
        zeroed = sem("zeroed")
        stacks_set = sem("stacks_set")
        set_up = sem("set_up")
        fold_full = sem("fold_full")
        fold_read = sem("fold_read")
        full = [sem(f"work_full{k}") for k in range(NBANK)]
        read = [sem(f"work_read{k}") for k in range(NBANK)]
        mx_full, mx_read = sem("mx_full"), sem("mx_read")
        sc_full, exp_done = sem("sc_full"), sem("exp_done")
        av_full, av_read = sem("av_full"), sem("av_read")
        high_done = sem2("high_done")
        mid_done = sem2("mid_done")
        split_done = sem2("split_done")
        mrest_done, mmid_done, msplit_done = sem2("mrest_done"), sem2("mmid_done"), sem2("msplit_done")
        bst1_done, mvimg_done = sem("bst1_done"), sem("mvimg_done")
        sq_done, e_done = sem("sq_done"), sem("e_done")
        rstdimg_done = sem("rstdimg_done")
        eps_added, epsy_added = sem2("eps_added"), sem("epsy_added")
        xd_done = sem("xd_done")
        xw_done, xg_done, xl_done = sem("xw_done"), sem("xg_done"), sem("xl_done")
        rden_done = sem2("rden_done")
        tok_kept, h1_done, h1_kept = sem("tok_kept"), sem("h1_done"), sem("h1_kept")
        bst_done, mv_done, rstd_done = sem2("bst_done"), sem2("mv_done"), sem2("rstd_done")
        xn_done = sem2("xn_done")
        h2b_done = sem("h2b_done")
        y_done = sem("y_done")
        bsty_done, mvy_done = sem("bsty_done"), sem("mvy_done")
        rstdy_done, yn_done, yg_done = sem("rstdy_done"), sem("yn_done"), sem("yg_done")
        res_done = sem("res_done")

        def tiles():
            return [(2 * b + T, b, T, ROWS[T]) for b in range(IMGS) for T in range(2)]

        block = ctx.enter_context(nc.Block())

        @block.sync
        def _(sp):
            sp.dma_start(const[:, :], consts).then_inc(const_in, 16)

            def load_x(u):
                sp.dma_start(xin[:].rearrange("p b c s -> p (b c s)"),
                             x[u].rearrange("p b c s -> p (b c s)") if isinstance(u, int)
                             else x[bass.ds(u, 1)].rearrange("o p b c s -> (o p) (b c s)")
                             ).then_inc(x_in, 16)

            def spill_parts(s, u):
                for g in range(3):
                    sp.wait_ge(split_done[s], 3 * u + g + 1)
                    if g < 2:
                        pieces = [(scratch[s][g], 0, P, 0, HG)]
                    else:
                        pieces = [(scratch[s][0], 0, DB, HG, HEADS), (scratch[s][1], DB, P, HG, HEADS)]
                    for dram, p0, p1, h0, h1_ in pieces:
                        for part in range(PARTS):
                            sp.dma_start(dram[part].rearrange("(e h) w -> e h w", h=HEADS)[:, h0:h1_, :],
                                         parts[s][p0:p1, g, part, :]).then_inc(parts_out[s], 16)

            def load_stack(s, o, stack, slots):
                src = scratch[s][o].rearrange("a (e h) w -> a e (h w)", h=HEADS)
                for j0, j1 in ((0, 3), (3, 5), (5, 6)):
                    assert len(set(slots[j0:j1])) in (1, j1 - j0)
                    if slots[j0] == slots[j1 - 1]:
                        rows = src[slots[j0]:slots[j0] + 1].broadcast_to((j1 - j0, DH, HEADS * W))
                    else:
                        rows = src[slots[j0]:slots[j1 - 1] + 1]
                    sp.dma_start(stack[DH * j0:DH * j1, :, :].rearrange("p h w -> p (h w)"), rows
                                 ).then_inc(stack_in[s], 16)

            def spill_max(s, u):
                sp.wait_ge(msplit_done[s], u + 1)
                sp.dma_start(scratch_max[s].rearrange("a h w -> h a w"), mparts[s][:]
                             ).then_inc(mparts_out[s], 16)

            def load_max(s, u):
                sp.wait_ge(mparts_out[s], 16 * (u + 1))
                sp.dma_start(stack_q[s][KM:P, :, :], scratch_max[s]).then_inc(mrows_in[s], 16)

            def load_stacks(s, u, core):
                sp.wait_ge(parts_out[s], SPILLS * (u + 1))
                if core is not None:
                    sp.wait_ge(sc_full, STEPS * (core + 1))
                load_stack(s, 0, stack_q[s], SLOT_Q)
                load_stack(s, 1, stack_k[s], SLOT_K)

            def store(u):
                sp.wait_ge(res_done, IMGS * (u + 1))
                for T in range(2):
                    dst = (out[u] if isinstance(u, int)
                           else out[bass.ds(u, 1)].rearrange("o b s d -> (o b) s d"))
                    sp.dma_start(dst[:, COLS[T], :].rearrange("b s d -> s b d"),
                                 res[0:ROWS[T], T::2, :]).then_inc(stored, 16)

            def body(B):
                i = B.i
                if B.e:
                    load_x(i + 2)
                if B.a:
                    load_stacks(0, i + 1, B.cores if B.c1 else None)
                if B.c3:
                    store(i - 2)
                if B.c2:
                    spill_max(1, i - 1)
                    load_max(1, i - 1)
                if B.c1:
                    spill_parts(1, i)
                    load_stacks(1, i, B.cores + 1 if B.c2 else None)
                if B.a:
                    spill_max(0, i + 1)
                    load_max(0, i + 1)
                if B.e:
                    spill_parts(0, i + 2)

            pipeline(nc.sync, units, body)
            sp.wait_ge(stored, 32 * units)

        @block.gpsimd
        def _(pool):
            for s in range(2):
                nc.gpsimd.memset(stack_q[s][KS:P, :, :], 0.0)
                nc.gpsimd.memset(stack_k[s][KS:P, :, :], 1.0).then_inc(stacks_set, 1)
            pool.wait_ge(const_in, 16)
            pool.wait_ge(stacks_set, 2)
            pool.wait_ge(zeroed, 2)
            nc.gpsimd.tensor_tensor(pos_bias[:], c("pos", 2), c("tokb", 2), ALU.add).then_inc(set_up, 1)

            def split(B, s, u, groups):
                for g in groups:
                    k, count = B.job(f"g{s + 1}_{g}")
                    if g == 0 and above(SPILLS * u):
                        pool.wait_ge(parts_out[s], SPILLS * u)
                    pool.wait_ge(read[k], count)
                    nc.gpsimd.tensor_tensor(parts[s][:, g, 1, :], rest[s][:, g, :],
                                            ones[:].broadcast_to((P, W)),
                                            ALU.mult).then_inc(mid_done[s], 1)
                    pool.wait_ge(mid_done[s], 3 * u + g + 1)
                    nc.gpsimd.tensor_tensor(parts[s][:, g, 2, :], rest[s][:, g, :], parts[s][:, g, 1, :],
                                            ALU.subtract).then_inc(split_done[s], 1)

            def image(t, b):
                return t[:, 2 * b:2 * b + 2, :]

            def inverse_deviations(u, aggregated, eps_added, done):
                pool.wait_ge(aggregated, NT * (u + 1))
                nc.gpsimd.tensor_tensor(var_eps[:], mv[:, :, 1], eps[:], ALU.add).then_inc(eps_added, 1)
                pool.wait_ge(eps_added, u + 1)
                nc.gpsimd.tensor_tensor(rstd[:], var_eps[:], minus_half[:], ALU.pow).then_inc(done, 1)

            def body(B):
                i = B.i
                if B.c3:
                    u = i - 2
                    if isinstance(u, int) and u == 0:
                        pool.wait_ge(fold_read, 1)
                    for b in range(IMGS):
                        k, count = B.job(f"down_{b}")
                        pool.wait_ge(read[k], count)
                        nc.gpsimd.tensor_tensor(image(y, b), image(down, b),
                                                down_b[:].unsqueeze(1).broadcast_to((P, 2, D)),
                                                ALU.add).then_inc(y_done, 1)
                    inverse_deviations(u, mvy_done, epsy_added, rstdy_done)
                    for b in range(IMGS):
                        pool.wait_ge(yn_done, NT * u + 2 * b + 2)
                        nc.gpsimd.tensor_tensor(image(yg, b), image(yn, b),
                                                c("gam").unsqueeze(1).broadcast_to((P, 2, D)),
                                                ALU.mult).then_inc(yg_done, 1)
                    if above(32 * u):
                        pool.wait_ge(stored, 32 * u)
                    for b in range(IMGS):
                        pool.wait_ge(yg_done, IMGS * u + b + 1)
                        nc.gpsimd.tensor_tensor(image(res, b), image(yg, b), image(h2b, b),
                                                ALU.add).then_inc(res_done, 1)
                if B.c1:
                    inverse_deviations(i, mv_done[0], eps_added[0], rstd_done[0])
                if B.a:
                    if B.c1:
                        pool.wait_ge(h1_done, IMGS * (i + 1))
                    nc.gpsimd.tensor_tensor(tok[:], tok_next[:], c("bv1").unsqueeze(1).broadcast_to((P, NT, D)),
                                            ALU.add).then_inc(tok_kept, 1)
                if B.c1:
                    split(B, 1, i, (0, 1, 2))
                if B.e:
                    k, count = B.job("mean")
                    pool.wait_ge(read[k], count)
                    for b in range(IMGS):
                        nc.gpsimd.tensor_tensor(image(xd, b), image(tok_next, b),
                                                mean_img[:, b:b + 1].unsqueeze(2).broadcast_to((P, 2, D)),
                                                ALU.subtract).then_inc(xd_done, 1)
                    for b in range(IMGS):
                        pool.wait_ge(xd_done, IMGS * (i + 2) + b + 1)
                        nc.gpsimd.tensor_tensor(image(xw, b), image(xd, b), lnw, ALU.mult).then_inc(xw_done, 1)
                    k, count = B.job("var")
                    pool.wait_ge(read[k], count)
                    nc.gpsimd.tensor_tensor(rstd_img[:], var_img[:], minus_half[:, 0:IMGS],
                                            ALU.pow).then_inc(rstdimg_done, 1)
                    pool.wait_ge(rstdimg_done, i + 3)
                    for b in range(IMGS):
                        pool.wait_ge(xw_done, IMGS * (i + 2) + b + 1)
                        nc.gpsimd.tensor_tensor(image(xg, b), image(xw, b),
                                                rstd_img[:, b:b + 1].unsqueeze(2).broadcast_to((P, 2, D)),
                                                ALU.mult).then_inc(xg_done, 1)
                    for b in range(IMGS):
                        pool.wait_ge(xg_done, IMGS * (i + 2) + b + 1)
                        nc.gpsimd.tensor_tensor(image(xl, b), image(xg, b), lnb, ALU.add).then_inc(xl_done, 1)
                    split(B, 0, i + 2, (0,))
                if B.c2:
                    inverse_deviations(i - 1, mv_done[1], eps_added[1], rstd_done[1])
                if B.e:
                    split(B, 0, i + 2, (1, 2))
                if B.c2:
                    for b in range(IMGS):
                        nc.gpsimd.tensor_tensor(image(h2b, b), image(h2, b),
                                                c("bet").unsqueeze(1).broadcast_to((P, 2, D)),
                                                ALU.add).then_inc(h2b_done, 1)
                if B.c1:
                    pool.wait_ge(h1_done, IMGS * (i + 1))
                    nc.gpsimd.tensor_tensor(h1[:], h1_next[:], ones[:].unsqueeze(2).broadcast_to((P, NT, D)),
                                            ALU.mult).then_inc(h1_kept, 1)

            pipeline(nc.gpsimd, units, body)

        @block.scalar
        def _(act):
            act.wait_ge(const_in, 16)

            def ffn_output(B, b):
                u = B.i - 2
                if b == 0 and above(IMGS * u):
                    act.wait_ge(y_done, IMGS * u)
                k, n = B.job(f"down_{b}")
                act.wait_ge(full[k], n)
                nc.scalar.copy(down[0:ROWS[0], 2 * b, :], work[k][0:ROWS[0], 0:D])
                nc.scalar.copy(down[0:ROWS[1], 2 * b + 1, :],
                               work[k][0:ROWS[1], D:2 * D]).then_inc(read[k], 1)

            def exponentials(number, between):
                def evacuate_values(q):
                    act.wait_ge(av_full, QUADS * number + q + 1)
                    nc.scalar.copy(attT[:, q, :], av_bank[q % 2][:, 0:S]).then_inc(av_read, 1)

                for q in range(QUADS):
                    if above(QUADS * number + q - 1):
                        act.wait_ge(av_full, QUADS * number + q - 1)
                    for j in range(4):
                        hp, T = j // 2, j % 2
                        step = 4 * q + j
                        act.wait_ge(sc_full, STEPS * number + step + 1)
                        nc.scalar.activation(
                            probs[0:ROWS[T], q % 2, T, 2 * hp:2 * hp + 2, :],
                            sc_bank[step % 2][0:ROWS[T], 0:2 * S].rearrange("p (h s) -> p h s", h=2),
                            ACT.Exp, scale=float(DH) ** -0.5).then_inc(exp_done, 1)
                        if j == 0 and q >= 2:
                            evacuate_values(q - 2)
                        between(step)
                evacuate_values(QUADS - 2)
                evacuate_values(QUADS - 1)

            def high_parts(B, s, u, groups):
                if 0 in groups and above(SPILLS * u):
                    act.wait_ge(parts_out[s], SPILLS * u)
                for g in groups:
                    k, n = B.job(f"g{s + 1}_{g}")
                    act.wait_ge(full[k], n)
                    nc.scalar.activation(parts[s][:, g, 0, :], work[k][:, 0:W], ACT.Identity,
                                         bias=group_b[s][:, g:g + 1]).then_inc(high_done[s], 1)

            def high_max(B, s, u):
                if above(16 * u):
                    act.wait_ge(mparts_out[s], 16 * u)
                k, n = B.job(f"mt{s + 1}")
                act.wait_ge(full[k], n)
                nc.scalar.mul(mparts[s][:, 0, :], work[k][0:HEADS, 0:W], -1.0)
                nc.scalar.mul(mneg[s][:], work[k][0:HEADS, 0:W], -1.0).then_inc(read[k], 1)

            def values(B, s):
                for b in range(IMGS):
                    k, n = B.job(f"v{s + 1}_{b}")
                    act.wait_ge(full[k], n)
                    for T in range(2):
                        R = ROWS[T]
                        last = nc.scalar.copy(
                            val[s][0:R, 2 * b + T, :, 0:DH],
                            work[k][0:R, T * D:(T + 1) * D].rearrange("p (h d) -> p h d", h=HEADS))
                    last.then_inc(read[k], 1)

            def evacuate(B, name, dst):
                for half, rows in enumerate((P, DB)):
                    k, n = B.job(f"{name}_{half}")
                    act.wait_ge(full[k], n)
                    nc.scalar.copy(dst[half][0:rows, :, :].rearrange("p b s -> p (b s)"),
                                   work[k][0:rows, 0:W]).then_inc(read[k], 1)

            def body(B):
                i = B.i

                def beside_1(step):
                    if B.c3 and step in (2, 3):
                        ffn_output(B, step - 2)

                def beside_2(step):
                    if B.c1 and step == 2:
                        high_parts(B, 1, i, (2,))

                if B.c1:
                    exponentials(B.cores, beside_1)
                elif B.c3:
                    beside_1(2)
                    beside_1(3)
                if B.c2:
                    high_max(B, 1, i - 1)
                if B.c1:
                    evacuate(B, "xt2", xT[1])
                    high_parts(B, 1, i, (0, 1))
                if B.c2:
                    exponentials(B.cores + int(B.c1), beside_2)
                elif B.c1:
                    beside_2(2)
                if B.a:
                    high_max(B, 0, i + 1)
                    values(B, 0)
                if B.e:
                    evacuate(B, "xt1", xT[0])
                if B.c2:
                    evacuate(B, "at", aT)
                if B.e:
                    high_parts(B, 0, i + 2, (0, 1, 2))
                if B.c1:
                    values(B, 1)
                if B.c2:
                    evacuate(B, "ft", fT)
                if B.c2:
                    k, n = B.job("up")
                    act.wait_ge(full[k], n)
                    nc.scalar.activation(hid[:].rearrange("p b s -> p (b s)"), work[k][:, 0:W],
                                         ACT.Relu).then_inc(read[k], 1)

            pipeline(nc.scalar, units, body)

        @block.vector
        def _(dve):
            for s in range(2):
                nc.vector.memset(val[s][:, :, :, 0:DH], 0.0)
                nc.vector.memset(val[s][:, :, :, DH:2 * DH], 1.0)
            for t in (xT[0][1], xT[1][1], aT[1], fT[1]):
                nc.vector.memset(t[DB:P, :, :], 0.0)
            for t in (mv_img, mv, tok_next, att, h2, down, yn):
                nc.vector.memset(t[:], 0.0)
            nc.vector.memset(probs[64:P, :, 1, :, :], 0.0)
            nc.vector.memset(eps[:], LN_EPS)
            nc.vector.memset(ones[:], 1.0)
            nc.vector.memset(minus_half[:], -0.5).then_inc(zeroed, 1)
            dve.wait_ge(zeroed, 1)
            for t in (xT[0][1], xT[1][1], aT[1], fT[1]):
                last = nc.vector.memset(t[DB:DB + 1, :, :], 1.0)
            last.then_inc(zeroed, 1)
            dve.wait_ge(const_in, 16)
            dve.wait_ge(fold_full, 2)
            nc.vector.tensor_copy(down_w[:], work[0][:, 0:D])
            nc.vector.tensor_copy(down_b[:], work[1][:, 0:D]).then_inc(fold_read, 1)
            dve.wait_ge(set_up, 1)

            def maxima(passes, step):
                q, j = divmod(step, 4)
                b, quad = divmod(q, QUADS // IMGS)
                hp, T = j // 2, j % 2
                h = 4 * quad + 2 * hp
                dve.wait_ge(mx_full, STEPS * passes + step + 1)
                nc.vector.tensor_reduce(
                    maxes[0:ROWS[T], 2 * b + T, h:h + 2],
                    mx_bank[step % 2][0:ROWS[T], 0:2 * S].rearrange("p (h s) -> p h s", h=2),
                    AX.X, ALU.max).then_inc(mx_read, 1)

            def normalise(B, s, u, b):
                for T, R in enumerate(ROWS):
                    n = 2 * b + T
                    k, count = B.job(f"ot{s + 1}_{n}")
                    dve.wait_ge(full[k], count)
                    nc.vector.reciprocal(
                        rden[0:R, n, :],
                        work[k][0:R, 0:2 * D].rearrange("p (h d) -> p h d", h=HEADS)[:, :, DH]
                    ).then_inc(rden_done[s], 1)
                for T, R in enumerate(ROWS):
                    n = 2 * b + T
                    k, count = B.job(f"ot{s + 1}_{n}")
                    dve.wait_ge(rden_done[s], NT * u + n + 1)
                    nc.vector.tensor_tensor(
                        att[0:R, n, :].rearrange("p (h d) -> p h d", h=HEADS),
                        work[k][0:R, 0:2 * D].rearrange("p (h d) -> p h d", h=HEADS)[:, :, 0:DH],
                        rden[0:R, n, :].unsqueeze(2).broadcast_to((R, HEADS, DH)),
                        ALU.mult).then_inc(read[k], 1)

            def max_rest(B, s, u):
                k, n = B.job(f"mt{s + 1}")
                dve.wait_ge(read[k], n)
                nc.vector.tensor_tensor(mrest[s][:], mneg[s][:], mparts[s][:, 0, :],
                                        ALU.subtract).then_inc(mrest_done[s], 1)

            def max_split(B, s, u):
                dve.wait_ge(mrest_done[s], u + 1)
                nc.vector.tensor_copy(mparts[s][:, 1, :], mrest[s][:]).then_inc(mmid_done[s], 1)
                dve.wait_ge(mmid_done[s], u + 1)
                nc.vector.tensor_tensor(mparts[s][:, 2, :], mrest[s][:], mparts[s][:, 1, :],
                                        ALU.subtract).then_inc(msplit_done[s], 1)

            def rests(B, s, u, groups):
                if 0 in groups and above(3 * u):
                    dve.wait_ge(split_done[s], 3 * u)
                for g in groups:
                    k, n = B.job(f"g{s + 1}_{g}")
                    dve.wait_ge(high_done[s], 3 * u + g + 1)
                    nc.vector.scalar_tensor_tensor(rest[s][:, g, :], work[k][:, 0:W],
                                                   group_b[s][:, g:g + 1], parts[s][:, g, 0, :],
                                                   ALU.add, ALU.subtract).then_inc(read[k], 1)

            def aggregate(stats_done, u, aggregate_tile, aggregated):
                dve.wait_ge(stats_done, NT * (u + 1))
                nc.vector.memset(spare[:], 0.0)
                for n, b, T, R in tiles():
                    aggregate_tile(n, b, T, R).then_inc(aggregated, 1)

            def row_statistics(src, u, stats_done, tiles_):
                for n, b, T, R in tiles_:
                    nc.vector.bn_stats(bst[0:R, n, :], src[0:R, n, :]).then_inc(stats_done, 1)

            def row_aggregates(u, stats_done, aggregated):
                aggregate(stats_done, u,
                          lambda n, b, T, R: nc.vector.bn_aggr(mv[0:R, n, :], bst[0:R, n, :]), aggregated)

            def row_norm(src, dst, done, tiles_):
                for n, b, T, R in tiles_:
                    nc.vector.tensor_scalar(dst[0:R, n, :], src[0:R, n, :], mv[0:R, n, 0:1],
                                            rstd[0:R, n:n + 1], ALU.subtract, ALU.mult).then_inc(done, 1)

            def output_rows(B, step):
                u = B.i - 2
                if step in (13, 15, 17, 19):
                    n = (step - 13) // 2
                    dve.wait_ge(y_done, IMGS * u + n // 2 + 1)
                    row_statistics(y, u, bsty_done, tiles()[n:n + 1])
                if step == 20:
                    row_aggregates(u, bsty_done, mvy_done)
                if step == STEPS - 1:
                    if above(IMGS * u):
                        dve.wait_ge(yg_done, IMGS * u)
                    dve.wait_ge(rstdy_done, u + 1)
                    row_norm(y, yn, yn_done, tiles())

            def embedded_images(B, step):
                i = B.i
                if step == 8:
                    k, count = B.job("mean")
                    dve.wait_ge(full[k], count)
                    nc.vector.tensor_copy(mean_img[:], work[k][:, 0:IMGS])
                    nc.vector.tensor_tensor(dev_img[:], mv_img[:, :, :, 0],
                                            work[k][:, 0:IMGS].unsqueeze(1).broadcast_to((P, 2, IMGS)),
                                            ALU.subtract).then_inc(read[k], 1)
                if step == 9:
                    k, count = B.job("mean")
                    dve.wait_ge(read[k], count)
                    nc.vector.tensor_tensor(sq_img[:], dev_img[:], dev_img[:], ALU.mult).then_inc(sq_done, 1)
                if step == 10:
                    dve.wait_ge(sq_done, i + 3)
                    nc.vector.tensor_tensor(e_img[:], sq_img[:], mv_img[:, :, :, 1],
                                            ALU.add).then_inc(e_done, 1)
                if step == 12:
                    k, count = B.job("var")
                    dve.wait_ge(full[k], count)
                    nc.vector.tensor_scalar(var_img[:], work[k][:, 0:IMGS], LN_EPS, None,
                                            ALU.add).then_inc(read[k], 1)
            def add_rows(B, name, b, dst, other):
                k, count = B.job(f"{name}_{b}")
                dve.wait_ge(full[k], count)
                for T in range(2):
                    R = ROWS[T]
                    last = nc.vector.tensor_tensor(dst[0:R, 2 * b + T, :], work[k][0:R, T * D:(T + 1) * D],
                                                   other(2 * b + T, T, R), ALU.add)
                last.then_inc(read[k], 1)

            def embedding(B, b):
                add_rows(B, "emb", b, tok_next, lambda n, T, R: pos_bias[0:R, T, :])
                k, count = B.job(f"emb_{b}")
                dve.wait_ge(read[k], count)
                for T in range(2):
                    n, R = 2 * b + T, ROWS[T]
                    nc.vector.bn_stats(bst1[0:R, n, :], tok_next[0:R, n, :]).then_inc(bst1_done, 1)

            def body(B):
                i = B.i
                for step in range(STEPS):
                    if B.c2 and step >= AHEAD:
                        maxima(B.passes, step)
                    if B.c3:
                        output_rows(B, step)
                if B.c1:
                    if above(i):
                        dve.wait_ge(h1_kept, i)
                    dve.wait_ge(tok_kept, i + 1)
                    for b in range(IMGS):
                        normalise(B, 0, i, b)
                        for n in (2 * b, 2 * b + 1):
                            k, count = B.job(f"ot1_{n}")
                            dve.wait_ge(read[k], count)
                        nc.vector.tensor_tensor(h1_next[:, 2 * b:2 * b + 2, :], att[:, 2 * b:2 * b + 2, :],
                                                tok[:, 2 * b:2 * b + 2, :], ALU.add).then_inc(h1_done, 1)
                        dve.wait_ge(h1_done, IMGS * i + b + 1)
                        row_statistics(h1_next, i, bst_done[0], tiles()[2 * b:2 * b + 2])
                    row_aggregates(i, bst_done[0], mv_done[0])
                if B.c2:
                    max_rest(B, 1, i - 1)
                    max_split(B, 1, i - 1)
                if B.c1:
                    dve.wait_ge(rstd_done[0], i + 1)
                    row_norm(h1_next, xn1, xn_done[0], tiles())
                if B.e:
                    if B.a:
                        dve.wait_ge(tok_kept, i + 2)
                    embedding(B, 0)
                if B.a:
                    maxima(B.passes + int(B.c2), 0)
                    maxima(B.passes + int(B.c2), 1)
                if B.e:
                    embedding(B, 1)
                    aggregate(bst1_done, i + 2,
                              lambda n, b, T, R: nc.vector.bn_aggr(mv_img[0:R, T, b, :], bst1[0:R, n, :]),
                              mvimg_done)
                if B.a:
                    for step in range(2, AHEAD):
                        maxima(B.passes + int(B.c2), step)
                if B.c1:
                    rests(B, 1, i, (0, 1))
                for step in range(STEPS):
                    if B.a and step >= AHEAD:
                        maxima(B.passes + int(B.c2), step)
                    if B.c1 and step == 9:
                        rests(B, 1, i, (2,))
                    if B.e:
                        embedded_images(B, step)
                if B.c2:
                    normalise(B, 1, i - 1, 0)
                    normalise(B, 1, i - 1, 1)
                if B.a:
                    max_rest(B, 0, i + 1)
                    max_split(B, 0, i + 1)
                if B.e:
                    rests(B, 0, i + 2, (0,))
                if B.c2:
                    u = i - 1
                    if above(IMGS * u):
                        dve.wait_ge(h2b_done, IMGS * u)
                    dve.wait_ge(h1_kept, i)
                    for b in range(IMGS):
                        add_rows(B, "proj", b, h2, lambda n, T, R: h1[0:R, n, :])
                        k, count = B.job(f"proj_{b}")
                        dve.wait_ge(read[k], count)
                        row_statistics(h2, u, bst_done[1], tiles()[2 * b:2 * b + 2])
                    row_aggregates(u, bst_done[1], mv_done[1])
                if B.e:
                    rests(B, 0, i + 2, (1, 2))
                if B.c1:
                    maxima(B.passes + int(B.c2) + int(B.a), 0)
                if B.c2:
                    dve.wait_ge(rstd_done[1], u + 1)
                    row_norm(h2, xn2, xn_done[1], tiles())
                if B.c1:
                    for step in range(1, AHEAD):
                        maxima(B.passes + int(B.c2) + int(B.a), step)

            pipeline(nc.vector, units, body)

        @block.tensor
        def _(pe):
            pe.wait_ge(const_in, 16)
            pe.wait_ge(zeroed, 2)

            for k, (name, n) in enumerate((("w2", INNER), ("b2", P))):
                for half in range(2):
                    last = nc.tensor.matmul(work[k][:, 0:D], c(name, 2)[:, half, :], c("wo", 2)[:, half, :],
                                            start=half == 0, stop=half == 1)
                last.then_inc(fold_full, 1)
            pe.wait_ge(fold_read, 1)

            def begin(B, name):
                k, n = B.job(name)
                if above(n - 1):
                    pe.wait_ge(read[k], n - 1)
                return k, work[k]

            def was_read(B, name):
                k, n = B.job(name)
                pe.wait_ge(read[k], n)

            def step_of(step):
                q, j = divmod(step, 4)
                b, quad = divmod(q, QUADS // IMGS)
                return b, 4 * quad + 2 * (j // 2), j % 2

            def part(stack, rows, h, b, cols):
                return stack[0:rows, h, b * S + cols.start:b * S + cols.stop]

            def for_maxima(maxima, step):
                s, u, number = maxima
                b, h0, T = step_of(step)
                if step == 0:
                    pe.wait_ge(stack_in[s], LOADS * (u + 1))
                if above(STEPS * number + step - 1):
                    pe.wait_ge(mx_read, STEPS * number + step - 1)
                for h in (0, 1):
                    last = nc.tensor.matmul(
                        mx_bank[step % 2][0:ROWS[T], h * S:(h + 1) * S],
                        part(stack_q[s], KM, h0 + h, b, COLS[T]),
                        part(stack_k[s], KM, h0 + h, b, slice(0, S)), start=True, stop=True)
                last.then_inc(mx_full, 1)

            def core(scores, maxima, between):
                for q in range(QUADS):
                    for j in range(4):
                        step = 4 * q + j
                        b, h0, T = step_of(step)
                        if maxima is not None and j > 0:
                            for_maxima(maxima, AHEAD + 3 * q + j - 1)
                        if scores is not None:
                            s, u, number, lent = scores
                            if step == 0:
                                pe.wait_ge(mrows_in[s], 16 * (u + 1))
                            if above(STEPS * number + step - 1):
                                pe.wait_ge(exp_done, STEPS * number + step - 1)
                            for h in (0, 1):
                                last = nc.tensor.matmul(
                                    sc_bank[step % 2][0:ROWS[T], h * S:(h + 1) * S],
                                    part(stack_k[s], P, h0 + h, b, COLS[T]),
                                    part(stack_q[s], P, h0 + h, b, slice(0, S)), start=True, stop=True)
                            last.then_inc(sc_full, 1)
                        if scores is not None and q > 0 and j % 2 == 1:
                            times_values(scores, q - 1, j // 2)
                        between(step)

            def times_values(scores, q, T):
                s, u, number, lent = scores
                b, quad = divmod(q, QUADS // IMGS)
                if T == 0:
                    pe.wait_ge(exp_done, STEPS * number + 4 * (q + 1))
                    if above(QUADS * number + q - 1):
                        pe.wait_ge(av_read, QUADS * number + q - 1)
                    if q == 1 and above(lent):
                        pe.wait_ge(read[LENT], lent)
                for h in range(4):
                    last = nc.tensor.matmul(av_bank[q % 2][2 * DH * h:2 * DH * (h + 1), 0:S],
                                            val[s][:, 2 * b + T, 4 * quad + h, :],
                                            probs[:, q % 2, T, h, :], start=T == 0, stop=T == 1)
                if T == 1:
                    last.then_inc(av_full, 1)

            def attention_rows(B, s, n):
                b, T = divmod(n, 2)
                k, ps = begin(B, f"ot{s + 1}_{n}")
                for quad in range(3):
                    last = nc.tensor.transpose(ps[0:ROWS[T], quad * P:(quad + 1) * P],
                                               attT[:, 3 * b + quad, COLS[T]], ident)
                last.then_inc(full[k], 1)

            def max_columns(B, s, passes):
                k, ps = begin(B, f"mt{s + 1}")
                pe.wait_ge(mx_read, STEPS * (passes + 1))
                for n, b, T, R in tiles():
                    last = nc.tensor.transpose(ps[0:HEADS, b * S + COLS[T].start:b * S + COLS[T].stop],
                                               maxes[0:R, n, :], ident[0:R, 0:R])
                last.then_inc(full[k], 1)

            def transposed(B, name, src, src_done):
                banks = [begin(B, f"{name}_{half}") for half in range(2)]
                for half, (k, ps) in enumerate(banks):
                    for n, b, T, R in tiles():
                        if half == 0:
                            src_done(n)
                        width = (P, DB)[half]
                        last = nc.tensor.transpose(ps[0:width, b * S + COLS[T].start:b * S + COLS[T].stop],
                                                   src[0:R, n, half * P:half * P + width],
                                                   ident[0:R, 0:R])
                    last.then_inc(full[k], 1)

            def groups(B, s, groups_):
                for g in groups_:
                    k, ps = begin(B, f"g{s + 1}_{g}")
                    halves = ([1] if g == 2 else [0]) if s == 0 else [0, 1]
                    for half in halves:
                        if g == 0 or (s == 0 and g == 2):
                            was_read(B, f"xt{2 if s else 1}_{half}")
                        last = nc.tensor.matmul(ps[:, 0:W], group_w[s][:, half, g * P:(g + 1) * P],
                                                xT[s][half][:].rearrange("p b s -> p (b s)"),
                                                start=half == halves[0], stop=half == halves[-1])
                    last.then_inc(full[k], 1)

            def rows_times(B, name, xT_, w, images=range(IMGS)):
                for b in images:
                    k, ps = begin(B, f"{name}_{b}")
                    for T in range(2):
                        for half in range(len(xT_)):
                            last = nc.tensor.matmul(ps[0:ROWS[T], T * D:(T + 1) * D],
                                                    xT_[half][:, b, COLS[T]], w[half],
                                                    start=half == 0, stop=half == len(xT_) - 1)
                    last.then_inc(full[k], 1)

            def values_1(B):
                for b in range(IMGS):
                    k, ps = begin(B, f"v1_{b}")
                    for T in range(2):
                        for half, (c0, c1) in enumerate(((0, P), (P, D))):
                            last = nc.tensor.matmul(ps[0:ROWS[T], T * D + c0:T * D + c1],
                                                    xT[0][half][:, b, COLS[T]],
                                                    value_w[0][:, half, c0:c1], start=True, stop=True)
                    last.then_inc(full[k], 1)

            def image_sum(B, name, rhs):
                k, ps = begin(B, name)
                for T in range(2):
                    last = nc.tensor.matmul(ps[:, 0:IMGS], avg[0:ROWS[T], :], rhs(T),
                                            start=T == 0, stop=T == 1)
                last.then_inc(full[k], 1)

            def embed(B, b, maxima):
                if B.e:
                    k, ps = begin(B, f"emb_{b}")
                for T in range(2):
                    for ch in range(CH):
                        if B.e:
                            last = nc.tensor.matmul(ps[0:ROWS[T], T * D:(T + 1) * D],
                                                    xin[:, b, ch, COLS[T]], wm[:, ch, :],
                                                    start=ch == 0, stop=ch == CH - 1)
                        if maxima is not None and (T, ch) in EMBED_MAXIMA:
                            for_maxima(maxima, EMBED_MAXIMA.index((T, ch)))
                if B.e:
                    last.then_inc(full[k], 1)

            def whole_core(B, s, scores, maxima, between):
                core(scores, maxima, between)
                if scores is not None:
                    quads = QUADS * scores[2]
                    pe.wait_ge(av_read, quads + QUADS // IMGS)
                    attention_rows(B, s, 0)
                    times_values(scores, QUADS - 1, 0)
                    times_values(scores, QUADS - 1, 1)
                    attention_rows(B, s, 1)
                    pe.wait_ge(av_read, quads + QUADS)
                if maxima is not None:
                    max_columns(B, 1 - s, maxima[2])
                if scores is not None:
                    attention_rows(B, s, 2)
                    attention_rows(B, s, 3)

            def body(B):
                i = B.i
                maxima_2 = (0, i + 1, B.passes + int(B.c2)) if B.a else None

                def ffn_output(step):
                    if B.c3 and step == 1:
                        k, n = B.last("up")
                        pe.wait_ge(read[k], n)
                        rows_times(B, "down", [hid], [down_w[:]])

                whole_core(B, 0, (0, i, B.cores, B.lent(0)) if B.c1 else None,
                           (1, i - 1, B.passes) if B.c2 else None, ffn_output)
                if B.e:
                    pe.wait_ge(x_in, 16 * (i + 3))
                    embed(B, 0, None)
                if B.a:
                    embed(B, 1, maxima_2)
                elif B.e:
                    embed(B, 1, None)
                if B.c1:
                    transposed(B, "xt2", xn1, lambda n: pe.wait_ge(xn_done[0], NT * i + n + 1))
                if B.c1:
                    groups(B, 1, (0,))
                if B.a:
                    for_maxima(maxima_2, 4)
                    for_maxima(maxima_2, 5)
                if B.c1:
                    groups(B, 1, (1,))

                def work_2(step):
                    if B.c1 and step == 1:
                        groups(B, 1, (2,))
                    if B.e and step == 2:
                        pe.wait_ge(mvimg_done, NT * (i + 3))
                        image_sum(B, "mean", lambda T: mv_img[0:ROWS[T], T, :, 0])
                    if B.e and step == 7:
                        pe.wait_ge(e_done, i + 3)
                        image_sum(B, "var", lambda T: e_img[0:ROWS[T], T, :])

                whole_core(B, 1, (1, i - 1, B.cores + int(B.c1), B.lent(1)) if B.c2 else None,
                           maxima_2, work_2)
                if B.a:
                    values_1(B)
                if B.e:
                    transposed(B, "xt1", xl, lambda n: pe.wait_ge(xl_done, IMGS * (i + 2) + n // 2 + 1))
                if B.c2:
                    transposed(B, "at", att, lambda n: was_read(B, f"ot2_{n}"))
                if B.e:
                    groups(B, 0, (0,))
                if B.c2:
                    was_read(B, "at_0")
                    was_read(B, "at_1")
                    rows_times(B, "proj", aT, [proj_w[:, 0, :], proj_w[:, 1, :]])
                if B.e:
                    groups(B, 0, (1, 2))
                maxima_1 = (1, i, B.passes + int(B.c2) + int(B.a))
                if B.c1:
                    weights = [value_w[1][:, 0, :], value_w[1][:, 1, :]]
                    rows_times(B, "v2", xT[1], weights, (0,))
                    for_maxima(maxima_1, 0)
                    for_maxima(maxima_1, 1)
                    rows_times(B, "v2", xT[1], weights, (1,))
                if B.c2:
                    u = i - 1
                    transposed(B, "ft", xn2, lambda n: pe.wait_ge(xn_done[1], NT * u + n + 1))
                if B.c1:
                    for step in range(2, AHEAD - 1):
                        for_maxima(maxima_1, step)
                if B.c2:
                    k, ps = begin(B, "up")
                    for half in range(2):
                        was_read(B, f"ft_{half}")
                        last = nc.tensor.matmul(ps[:, 0:W], up_w[:, half, :],
                                                fT[half][:].rearrange("p b s -> p (b s)"),
                                                start=half == 0, stop=half == 1)
                    last.then_inc(full[k], 1)
                if B.c1:
                    for_maxima(maxima_1, AHEAD - 1)

            pipeline(nc.tensor, units, body)


def kernel(x, L0_tok_W_map, L0_tok_b_map, L0_tok_class_token, L0_tok_ln_w, L0_tok_ln_b, L0_tok_Wq,
           L0_tok_bq, L0_tok_Wk, L0_tok_bk, L0_tok_Wv, L0_tok_bv, L0_attn_w_attn, L0_attn_b_attn,
           L0_attn_w_proj, L0_attn_b_proj, L0_ffn_W1, L0_ffn_b1, L0_ffn_W2, L0_ffn_b2, L0_ffn_Wo,
           L0_ffn_bo, L0_ffn_gamma, L0_ffn_beta):
    import numpy as np
    import concourse.bacc as bacc
    from concourse.bass_utils import run_bass_kernel_spmd

    f32 = np.float32
    images = np.asarray(x)
    units = images.shape[0] // IMGS

    patches = images.reshape(units, IMGS, S - 1, CH, P)
    x_host = np.zeros((units, P, IMGS, CH, S), f32)
    x_host[..., 1:] = patches.transpose(0, 4, 1, 3, 2)

    packed = np.zeros((P, NCONST), f32)

    def put(name, value):
        at, n = CONST[name]
        value = np.asarray(value)
        chunks = value[None] if value.ndim == 2 else value
        per = n // len(chunks)
        for k, v in enumerate(chunks):
            packed[:v.shape[0], at + k * per:at + k * per + v.shape[1]] = v

    def row_tiles(a):
        t = np.zeros((2, P, D), f32)
        t[0], t[1, :S - P] = a[:P], a[P:]
        return t

    def contraction(a, bias=None):
        t = np.zeros((2, P, a.shape[1]), f32)
        t[0], t[1, :DB] = a[:P], a[P:]
        if bias is not None:
            t[1, DB] = bias
        return t

    def blocks(w):
        t = np.zeros((D, D), f32)
        for h in range(HEADS):
            t[h * DH:(h + 1) * DH, h * DH:(h + 1) * DH] = w[h].T
        return t

    def grouped(q, k):
        def heads(a, h0, h1):
            a = a.reshape(a.shape[:-1] + (HEADS, DH))[..., h0:h1, :]
            return np.swapaxes(a, -1, -2).reshape(a.shape[:-2] + (-1,))
        return np.concatenate([heads(q, 0, HG), heads(k, 0, HG), heads(q, HG, HEADS),
                               heads(k, HG, HEADS)], axis=-1)

    i = np.arange(S, dtype=f32)[:, None]
    j = np.arange(D, dtype=f32)[None, :]
    pos = np.where((np.arange(D) % 2 == 0)[None, :], np.sin(i / np.power(f32(10000.0), j / f32(D))),
                   np.cos(i / np.power(f32(10000.0), (j - f32(1.0)) / f32(D)))).astype(f32)
    tokb = np.zeros((S, D), f32)
    tokb[0], tokb[1:] = np.asarray(L0_tok_class_token)[0], np.asarray(L0_tok_b_map)

    wq, wk, wv = (blocks(np.asarray(w)) for w in (L0_tok_Wq, L0_tok_Wk, L0_tok_Wv))
    w_attn, b_attn = np.asarray(L0_attn_w_attn), np.asarray(L0_attn_b_attn)

    put("wm", np.asarray(L0_tok_W_map).T.reshape(CH, P, D))
    put("pos", row_tiles(pos))
    put("tokb", row_tiles(tokb))
    put("lnw", row_tiles(np.asarray(L0_tok_ln_w)))
    put("lnb", row_tiles(np.asarray(L0_tok_ln_b)))
    put("g1", contraction(grouped(wq, wk)))
    put("g2", contraction(grouped(w_attn[:, :D], w_attn[:, D:2 * D])))
    put("gb1", grouped(np.asarray(L0_tok_bq).reshape(D), np.asarray(L0_tok_bk).reshape(D)).reshape(3, P).T)
    put("gb2", grouped(b_attn[:D], b_attn[D:2 * D]).reshape(3, P).T)
    put("wv1", contraction(wv))
    put("bv1", np.broadcast_to(np.asarray(L0_tok_bv).reshape(D), (P, D)))
    put("wv2", contraction(w_attn[:, 2 * D:], b_attn[2 * D:]))
    put("wp", contraction(np.asarray(L0_attn_w_proj), np.asarray(L0_attn_b_proj)))
    put("w1", contraction(np.asarray(L0_ffn_W1).T, np.asarray(L0_ffn_b1)))
    put("w2", contraction(np.asarray(L0_ffn_W2)))
    put("wo", contraction(np.asarray(L0_ffn_Wo).T, np.asarray(L0_ffn_bo)))
    put("b2", contraction(np.broadcast_to(np.asarray(L0_ffn_b2)[:, None], (D, P)), np.ones(P, f32)))
    put("gam", np.broadcast_to(np.asarray(L0_ffn_gamma), (P, D)))
    put("bet", np.broadcast_to(np.asarray(L0_ffn_beta), (P, D)))
    put("ident", np.eye(P, dtype=f32))
    put("avg", np.full((P, P), 1.0 / S, f32))

    nc = bacc.Bacc("TRN2", target_bir_lowering=False, num_devices=1)
    x_dram = nc.dram_tensor("x_dram", x_host.shape, F32, kind="ExternalInput").ap()
    const_dram = nc.dram_tensor("const_dram", packed.shape, F32, kind="ExternalInput").ap()
    out_dram = nc.dram_tensor("out_dram", (units, IMGS, S, D), F32, kind="ExternalOutput").ap()
    vit_tower(nc, x_dram, const_dram, out_dram)
    result = run_bass_kernel_spmd(nc, [{"x_dram": x_host, "const_dram": packed}], core_ids=[0])
    return result.results[0]["out_dram"].reshape(images.shape[0], S, D)
```
